# Optimizing a Trainium2 kernel written in Bass

```python
import numpy as np
import jax
import jax.numpy as jnp

def _softmax(x, axis=-1):
    return jax.nn.softmax(x, axis=axis)

def _gelu(x):
    return jax.nn.gelu(x, approximate=True)

def _silu(x):
    return jax.nn.silu(x)

def _sigmoid(x):
    return jax.nn.sigmoid(x)

def _layernorm(x, axis=-1, eps=1e-05):
    m = jnp.mean(x, axis=axis, keepdims=True)
    v = jnp.var(x, axis=axis, keepdims=True)
    return (x - m) / jnp.sqrt(v + eps)

def _scatter_add(tgt, idx, src, axis=0):
    return tgt.at[idx].add(src)

def _segment_sum(src, seg, n):
    return jax.ops.segment_sum(src, seg, n)
kernel_name = 'mk_macaron_d1_jaxref_r8_ff24c4'

def setup_inputs(seed: int=0):
    np.random.seed(seed)
    _w = jnp.asarray

    def _L0_attn_setup():
        import jax, jax.numpy as jnp
        import numpy as np
        from jax import lax
        BATCH = 2
        SEQ = 256
        HID = 256
        EXPAND = 2
        INTER = EXPAND * HID
        HEADS = 64
        PDIM = INTER // HEADS
        NSTATE = 128
        G = 1
        HPG = HEADS // G
        KCONV = 4
        GTS = G * NSTATE
        CONV_DIM = INTER + 2 * GTS
        PROJ_DIM = 2 * INTER + 2 * GTS + HEADS
        EPS = 1e-05
        MUP = (0.25, 0.5, 0.5, 0.5, 1.0)

        def _mup_vector():
            return jnp.concatenate([jnp.full((INTER,), MUP[0], jnp.float32), jnp.full((INTER,), MUP[1], jnp.float32), jnp.full((GTS,), MUP[2], jnp.float32), jnp.full((GTS,), MUP[3], jnp.float32), jnp.full((HEADS,), MUP[4], jnp.float32)])

        def _forward(hidden_states, in_proj_w, conv_w, conv_b, A_log, D, dt_bias, norm_w, out_proj_w):
            b, l, _ = hidden_states.shape
            proj = hidden_states @ in_proj_w * _mup_vector()
            z = proj[..., :INTER]
            xBC = proj[..., INTER:INTER + CONV_DIM]
            dt = proj[..., INTER + CONV_DIM:]
            xBC_cl = jnp.swapaxes(xBC, 1, 2)
            conv = lax.conv_general_dilated(xBC_cl, conv_w[:, None, :], window_strides=(1,), padding=((KCONV - 1, 0),), feature_group_count=CONV_DIM)
            xBC = jax.nn.silu(jnp.swapaxes(conv + conv_b[None, :, None], 1, 2))
            x = xBC[..., :INTER].reshape(b, l, G, HPG, PDIM)
            Bm = xBC[..., INTER:INTER + GTS].reshape(b, l, G, NSTATE)
            Cm = xBC[..., INTER + GTS:].reshape(b, l, G, NSTATE)
            dt = jax.nn.softplus(dt + dt_bias)
            A = -jnp.exp(A_log)
            dA = jnp.exp(dt * A).reshape(b, l, G, HPG)
            dtx = dt.reshape(b, l, G, HPG)[..., None] * x

            def step(state, inp):
                dA_t, dtx_t, B_t, C_t = inp
                state = state * dA_t[..., None, None] + jnp.einsum('bgcp,bgn->bgcpn', dtx_t, B_t)
                y_t = jnp.einsum('bgn,bgcpn->bgcp', C_t, state)
                return (state, y_t)
            inputs = (jnp.moveaxis(dA, 1, 0), jnp.moveaxis(dtx, 1, 0), jnp.moveaxis(Bm, 1, 0), jnp.moveaxis(Cm, 1, 0))
            state0 = jnp.zeros((b, G, HPG, PDIM, NSTATE), hidden_states.dtype)
            _, ys = lax.scan(step, state0, inputs)
            y = jnp.moveaxis(ys, 0, 1) + D.reshape(1, 1, G, HPG, 1) * x
            y = y.reshape(b, l, INTER)
            yg = y.reshape(b, l, G, INTER // G)
            var = jnp.mean(jnp.square(yg), axis=-1, keepdims=True)
            yn = (yg * lax.rsqrt(var + EPS)).reshape(b, l, INTER) * norm_w
            out = yn * jax.nn.silu(z)
            return out @ out_proj_w
        key = jax.random.key(seed)
        ks = jax.random.split(key, 8)
        hidden_states = jax.random.normal(ks[0], (BATCH, SEQ, HID), jnp.float32)
        in_proj_w = jax.random.normal(ks[1], (HID, PROJ_DIM), jnp.float32) * 0.02
        conv_w = jax.random.normal(ks[2], (CONV_DIM, KCONV), jnp.float32) * 0.2
        conv_b = jnp.zeros((CONV_DIM,), jnp.float32)
        A_log = jnp.log(jnp.arange(1, HEADS + 1, dtype=jnp.float32))
        D = jnp.ones((HEADS,), jnp.float32)
        dt_bias = jax.random.uniform(ks[3], (HEADS,), jnp.float32)
        norm_w = jnp.ones((INTER,), jnp.float32)
        out_proj_w = jax.random.normal(ks[4], (INTER, HID), jnp.float32) * 0.02
        return dict(hidden_states=hidden_states, in_proj_w=in_proj_w, conv_w=conv_w, conv_b=conv_b, A_log=A_log, D=D, dt_bias=dt_bias, norm_w=norm_w, out_proj_w=out_proj_w)
    _L0_attn_in = _L0_attn_setup()

    def _L0_ffn_setup():
        import jax, jax.numpy as jnp
        import numpy as np
        HIDDEN = 256
        INTER = 688
        LUT_SIZE = 16

        def _ghost_linear(x, idx, lut):
            w = lut[idx]
            return jnp.einsum('bsh,oh->bso', x, w)
        key = jax.random.key(seed)
        k_x, k_lut, k_g, k_u, k_d = jax.random.split(key, 5)
        x = jax.random.normal(k_x, (2, 512, HIDDEN), dtype=jnp.float32)
        lut = jax.random.normal(k_lut, (LUT_SIZE,), dtype=jnp.float32) * 0.02
        gate_idx = jax.random.randint(k_g, (INTER, HIDDEN), 0, LUT_SIZE, dtype=jnp.int32)
        up_idx = jax.random.randint(k_u, (INTER, HIDDEN), 0, LUT_SIZE, dtype=jnp.int32)
        down_idx = jax.random.randint(k_d, (HIDDEN, INTER), 0, LUT_SIZE, dtype=jnp.int32)
        return {'x': x, 'lut': lut, 'gate_idx': gate_idx, 'up_idx': up_idx, 'down_idx': down_idx}
    _L0_ffn_in = _L0_ffn_setup()
    _d = {'L0_attn_hidden_states': _L0_attn_in['hidden_states'], 'L0_attn_in_proj_w': _L0_attn_in['in_proj_w'], 'L0_attn_conv_w': _L0_attn_in['conv_w'], 'L0_attn_conv_b': _L0_attn_in['conv_b'], 'L0_attn_A_log': _L0_attn_in['A_log'], 'L0_attn_D': _L0_attn_in['D'], 'L0_attn_dt_bias': _L0_attn_in['dt_bias'], 'L0_attn_norm_w': _L0_attn_in['norm_w'], 'L0_attn_out_proj_w': _L0_attn_in['out_proj_w'], 'L0_ffn_lut': _L0_ffn_in['lut'], 'L0_ffn_gate_idx': _L0_ffn_in['gate_idx'], 'L0_ffn_up_idx': _L0_ffn_in['up_idx'], 'L0_ffn_down_idx': _L0_ffn_in['down_idx']}
    _x0 = _d['L0_attn_hidden_states']
    _d['L0_attn_hidden_states'] = jax.random.normal(jax.random.fold_in(jax.random.key(seed), 1), (1, 2048, 256), dtype=_x0.dtype)
    del _x0
    return _d

def reference(L0_attn_hidden_states, L0_attn_in_proj_w, L0_attn_conv_w, L0_attn_conv_b, L0_attn_A_log, L0_attn_D, L0_attn_dt_bias, L0_attn_norm_w, L0_attn_out_proj_w, L0_ffn_lut, L0_ffn_gate_idx, L0_ffn_up_idx, L0_ffn_down_idx):

    def _L0_attn_ref(hidden_states, in_proj_w, conv_w, conv_b, A_log, D, dt_bias, norm_w, out_proj_w):
        import jax, jax.numpy as jnp
        import numpy as np
        from jax import lax
        BATCH = 2
        SEQ = 256
        HID = 256
        EXPAND = 2
        INTER = EXPAND * HID
        HEADS = 64
        PDIM = INTER // HEADS
        NSTATE = 128
        G = 1
        HPG = HEADS // G
        KCONV = 4
        GTS = G * NSTATE
        CONV_DIM = INTER + 2 * GTS
        PROJ_DIM = 2 * INTER + 2 * GTS + HEADS
        EPS = 1e-05
        MUP = (0.25, 0.5, 0.5, 0.5, 1.0)

        def _mup_vector():
            return jnp.concatenate([jnp.full((INTER,), MUP[0], jnp.float32), jnp.full((INTER,), MUP[1], jnp.float32), jnp.full((GTS,), MUP[2], jnp.float32), jnp.full((GTS,), MUP[3], jnp.float32), jnp.full((HEADS,), MUP[4], jnp.float32)])

        def _forward(hidden_states, in_proj_w, conv_w, conv_b, A_log, D, dt_bias, norm_w, out_proj_w):
            b, l, _ = hidden_states.shape
            proj = hidden_states @ in_proj_w * _mup_vector()
            z = proj[..., :INTER]
            xBC = proj[..., INTER:INTER + CONV_DIM]
            dt = proj[..., INTER + CONV_DIM:]
            xBC_cl = jnp.swapaxes(xBC, 1, 2)
            conv = lax.conv_general_dilated(xBC_cl, conv_w[:, None, :], window_strides=(1,), padding=((KCONV - 1, 0),), feature_group_count=CONV_DIM)
            xBC = jax.nn.silu(jnp.swapaxes(conv + conv_b[None, :, None], 1, 2))
            x = xBC[..., :INTER].reshape(b, l, G, HPG, PDIM)
            Bm = xBC[..., INTER:INTER + GTS].reshape(b, l, G, NSTATE)
            Cm = xBC[..., INTER + GTS:].reshape(b, l, G, NSTATE)
            dt = jax.nn.softplus(dt + dt_bias)
            A = -jnp.exp(A_log)
            dA = jnp.exp(dt * A).reshape(b, l, G, HPG)
            dtx = dt.reshape(b, l, G, HPG)[..., None] * x

            def step(state, inp):
                dA_t, dtx_t, B_t, C_t = inp
                state = state * dA_t[..., None, None] + jnp.einsum('bgcp,bgn->bgcpn', dtx_t, B_t)
                y_t = jnp.einsum('bgn,bgcpn->bgcp', C_t, state)
                return (state, y_t)
            inputs = (jnp.moveaxis(dA, 1, 0), jnp.moveaxis(dtx, 1, 0), jnp.moveaxis(Bm, 1, 0), jnp.moveaxis(Cm, 1, 0))
            state0 = jnp.zeros((b, G, HPG, PDIM, NSTATE), hidden_states.dtype)
            _, ys = lax.scan(step, state0, inputs)
            y = jnp.moveaxis(ys, 0, 1) + D.reshape(1, 1, G, HPG, 1) * x
            y = y.reshape(b, l, INTER)
            yg = y.reshape(b, l, G, INTER // G)
            var = jnp.mean(jnp.square(yg), axis=-1, keepdims=True)
            yn = (yg * lax.rsqrt(var + EPS)).reshape(b, l, INTER) * norm_w
            out = yn * jax.nn.silu(z)
            return out @ out_proj_w
        return _forward(hidden_states, in_proj_w, conv_w, conv_b, A_log, D, dt_bias, norm_w, out_proj_w)

    def _L0_ffn_ref(x, lut, gate_idx, up_idx, down_idx):
        import jax, jax.numpy as jnp
        import numpy as np
        HIDDEN = 256
        INTER = 688
        LUT_SIZE = 16

        def _ghost_linear(x, idx, lut):
            w = lut[idx]
            return jnp.einsum('bsh,oh->bso', x, w)
        gate = _ghost_linear(x, gate_idx, lut)
        up = _ghost_linear(x, up_idx, lut)
        h = jax.nn.silu(gate) * up
        return _ghost_linear(h, down_idx, lut)
    x = L0_attn_hidden_states
    x = x + 0.5 * _L0_ffn_ref(_layernorm(x, axis=-1), L0_ffn_lut, L0_ffn_gate_idx, L0_ffn_up_idx, L0_ffn_down_idx)
    x = x + _L0_attn_ref(_layernorm(x, axis=-1), L0_attn_in_proj_w, L0_attn_conv_w, L0_attn_conv_b, L0_attn_A_log, L0_attn_D, L0_attn_dt_bias, L0_attn_norm_w, L0_attn_out_proj_w)
    x = x + 0.5 * _L0_ffn_ref(_layernorm(x, axis=-1), L0_ffn_lut, L0_ffn_gate_idx, L0_ffn_up_idx, L0_ffn_down_idx)
    return x

_drawn_inputs = setup_inputs


def setup_inputs(seed=0):
    import zlib

    import numpy as np

    out = dict(_drawn_inputs(seed))
    spreads = {'L0_attn_conv_b': (0.0, 0.442), 'L0_attn_D': (1.0, 0.6), 'L0_attn_norm_w': (1.0, 0.6)}
    factors = {'L0_attn_in_proj_w': 3.021,
     'L0_attn_conv_w': 5.586,
     'L0_attn_A_log': 8.0,
     'L0_attn_dt_bias': 8.0,
     'L0_attn_out_proj_w': 3.012}
    for name, (base, spread) in spreads.items():
        noise = np.random.default_rng([zlib.crc32(name.encode()), seed]).standard_normal(out[name].shape)
        drawn = base * np.exp(spread * noise) if base else spread * noise
        out[name] = jnp.asarray(drawn.astype(out[name].dtype))
    for name, factor in factors.items():
        out[name] = (out[name] * factor).astype(out[name].dtype)
    return out
```

```python
from contextlib import ExitStack

import concourse.bass as bass
from concourse import mybir

F32 = mybir.dt.float32
F32R = mybir.dt.float32r
I32 = mybir.dt.int32
ALU = mybir.AluOpType
ACT = mybir.ActivationFunctionType

P = 128
L = 2048
HID = 256
KC = HID // P
TILES = L // P
GT = 4
GROUPS = TILES // GT
GN = GT * P
FF = 688
FCH = 6
FLAST = FF - 5 * P
LUT = 16
INTER = 512
HEADS = 64
PD = INTER // HEADS
NS = 128
KCONV = 4
CONV = INTER + 2 * NS
PROJ = 2 * INTER + 2 * NS + HEADS
PCH = 11
XCH = CONV // P
Q = 32
NB = P // Q
BLOCKS = L // Q
HG = 16
EPS = 1e-5
MUP_Z, MUP_X = 0.25, 0.5
GUC = 11
WCOLS = GUC * HID + 2 * FF
POOL_COLS = 1280


def split_mm(pe, out, w_hi, w_lo, x_hi, x_lo, start, stop):
    pe.matmul(out, w_hi, x_hi, start=start, stop=False)
    pe.matmul(out, w_hi, x_lo, start=False, stop=False)
    return pe.matmul(out, w_lo, x_hi, start=False, stop=stop)


def build_weights(nc, T, A):
    with ExitStack() as ctx:
        sb = lambda n, s, d=F32: ctx.enter_context(nc.sbuf_tensor(n, s, d))
        sem = lambda n: ctx.enter_context(nc.semaphore(n))
        idx = sb("idx", [P, WCOLS], I32)
        w_nat = sb("w_nat", [P, WCOLS])
        idxf = sb("idxf", [P, WCOLS])
        eq_v = sb("eq_v", [P, WCOLS - POOL_COLS])
        eq_p = sb("eq_p", [P, POOL_COLS])
        lut = sb("lut_bc", [P, LUT])
        win_raw = sb("win_raw", [P, KC, PROJ])
        wout_raw = sb("wout_raw", [P, 4, HID])
        tp = ctx.enter_context(nc.psum_tensor("w_tp", [P, 8, 512], F32))
        idx_pad, idx_in, lut_in, win_in, wout_in = map(sem, ("idx_pad", "idx_in", "lut_in", "win_in", "wout_in"))
        idxf_done, eqv, accv, eqp, accp = map(sem, ("idxf_done", "eqv", "accv", "eqp", "accp"))
        zeroed, split_hi, split_lo, ident_ok = map(sem, ("zeroed", "split_hi", "split_lo", "ident_ok"))
        tp_done, tp_hi, tp_lo, x_in, nw_in, wout_s = map(sem, ("tp_done", "tp_hi", "tp_lo", "x_in", "nw_in", "wout_s"))
        gu_idx = idx[:, 0:GUC * HID].rearrange("p (c h) -> p c h", c=GUC)
        dn_idx = idx[:, GUC * HID:].rearrange("p (c h) -> p c h", c=2)
        gu_nat = w_nat[:, 0:GUC * HID].rearrange("p (c h) -> p c h", c=GUC)
        dn_nat = w_nat[:, GUC * HID:].rearrange("p (c h) -> p c h", c=2)
        wgu = T["wgu"]
        wd = T["wd"]
        jobs, evacs = [], []
        n = 0
        for kc in range(KC):
            for c0 in range(0, GUC, 4):
                cs = list(range(c0, min(c0 + 4, GUC)))
                jobs.append([(tp[:, n % 8, 128 * j:128 * j + 128], gu_nat[:, c, P * kc:P * kc + P])
                             for j, c in enumerate(cs)])
                src = tp[:, n % 8, 0:128 * len(cs)]
                evacs.append((src, wgu[:, 0, kc, c0:c0 + len(cs), :].rearrange("p c n -> p (c n)"),
                              wgu[:, 1, kc, c0:c0 + len(cs), :].rearrange("p c n -> p (c n)")))
                n += 1
        for f0 in range(0, 4, 2):
            jobs.append([(tp[:, n % 8, 256 * j + 128 * m:256 * j + 128 * m + 128],
                          dn_nat[:, m, P * (f0 + j):P * (f0 + j) + P]) for j in range(2) for m in range(2)])
            evacs.append((tp[:, n % 8, :], wd[:, 0, f0:f0 + 2, :].rearrange("p c n -> p (c n)"),
                          wd[:, 1, f0:f0 + 2, :].rearrange("p c n -> p (c n)")))
            n += 1
        jobs.append([(tp[:, n % 8, 128 * m:128 * m + 128], dn_nat[:, m, P * 4:P * 5]) for m in range(2)])
        evacs.append((tp[:, n % 8, 0:256], wd[:, 0, 4, :], wd[:, 1, 4, :]))
        n += 1
        jobs.append([(tp[0:FLAST, n % 8, 128 * m:128 * m + 128], dn_nat[:, m, P * 5:FF]) for m in range(2)])
        evacs.append((tp[0:FLAST, n % 8, 0:256], wd[0:FLAST, 0, 5, :], wd[0:FLAST, 1, 5, :]))

        block = ctx.enter_context(nc.Block())
        v_cols = slice(0, WCOLS - POOL_COLS)
        p_cols = slice(WCOLS - POOL_COLS, WCOLS)

        @block.sync
        def _(sp):
            sp.dma_start(lut[:, :], A["lut"].unsqueeze(0).broadcast_to([P, LUT])).then_inc(lut_in, 16)
            for r, (name, c0) in enumerate((("gate", 0), ("up", 5))):
                sp.dma_start(gu_idx[:, c0:c0 + 5, :],
                             A[name][0:5 * P, :].rearrange("(c p) h -> p c h", p=P)).then_inc(idx_in, 16)
            sp.wait_ge(idx_pad, 1)
            sp.dma_start(gu_idx[0:FLAST, 10, :], A["gate"][5 * P:FF, :]).then_inc(idx_in, 16)
            sp.dma_start(gu_idx[64:64 + FLAST, 10, :], A["up"][5 * P:FF, :]).then_inc(idx_in, 16)
            sp.dma_start(dn_idx, A["down"].rearrange("(c p) f -> p c f", p=P)).then_inc(idx_in, 16)
            sp.dma_start(T["x_res"][:, :, :], A["x"][0].rearrange("(t p) c -> p t c", p=P)).then_inc(x_in, 16)
            sp.dma_start(win_raw[:, :, :], A["in_w"].rearrange("(k p) n -> p k n", p=P)).then_inc(win_in, 16)
            sp.dma_start(wout_raw[:, :, :], A["out_w"].rearrange("(k p) n -> p k n", p=P)).then_inc(wout_in, 16)
            with nc.allow_non_contiguous_dma(reason="per-channel vectors, small"):
                sp.dma_start(T["norm_w"][:, :], A["norm_w"].rearrange("(k p) -> p k", p=P)).then_inc(nw_in, 16)
                sp.dma_start(T["conv_b"][:, :], A["conv_b"].rearrange("(k p) -> p k", p=P)).then_inc(nw_in, 16)
                sp.dma_start(T["conv_w"][:, :, :], A["conv_w"].rearrange("(k p) j -> p k j", p=P)).then_inc(nw_in, 16)
                sp.dma_start(T["a_log"][:, :], A["A_log"].unsqueeze(1)).then_inc(nw_in, 16)
                sp.dma_start(T["dt_b"][:, :], A["dt_bias"].unsqueeze(1)).then_inc(nw_in, 16)
                for hh in range(HG):
                    sp.dma_start(T["d_ch"][PD * hh:PD * hh + PD, :],
                                 A["D"].rearrange("(g h) -> h g", h=HG)[hh:hh + 1, :].broadcast_to([PD, 4])
                                 ).then_inc(nw_in, 16)
            sp.wait_ge(x_in, 16)
            sp.wait_ge(nw_in, 16 * (5 + HG))

        @block.gpsimd
        def _(pool):
            pool.memset(gu_idx[:, 10, :], LUT).then_inc(idx_pad, 1)
            pool.memset(T["ident"][:, :], 0.0).then_inc(ident_ok, 1)
            pool.wait_ge(ident_ok, 1)
            pool.affine_select(out=T["ident"][:, :], in_=T["ident"][:, :], compare_op=ALU.not_equal, fill=1.0,
                               base=0, pattern=[[-1, P]], channel_multiplier=1).then_inc(ident_ok, 1)
            pool.memset(T["ones"][:, :], 1.0)
            pool.memset(T["m_half"][:, :], -0.5)
            for hl in range(2):
                pool.memset(T["wd"][:, hl, FCH - 1, :].bitcast(F32), 0.0).then_inc(zeroed, 1)
                pool.memset(T["win"][:, hl, :, PCH - 1, :].bitcast(F32), 0.0).then_inc(zeroed, 1)
            pool.wait_ge(lut_in, 16)
            pool.wait_ge(idxf_done, 2)
            pool.memset(w_nat[:, p_cols], 0.0).then_inc(accp, 1)
            for k in range(LUT):
                pool.wait_ge(accp, k + 1)
                pool.tensor_scalar(eq_p[:, :], idxf[:, p_cols], float(k), lut[:, k:k + 1],
                                   ALU.is_equal, ALU.mult).then_inc(eqp, 1)
                pool.wait_ge(eqp, k + 1)
                pool.tensor_tensor(w_nat[:, p_cols], w_nat[:, p_cols], eq_p[:, :], ALU.add).then_inc(accp, 1)
            pool.wait_ge(split_hi, 1)
            pool.tensor_tensor(T["win"][:, 1, :, :, :].rearrange("p k c n -> p k (c n)")[:, :, 0:PROJ],
                               win_raw[:, :, :],
                               T["win"][:, 0, :, :, :].rearrange("p k c n -> p k (c n)")[:, :, 0:PROJ].bitcast(F32),
                               ALU.subtract).then_inc(split_lo, 1)

        @block.vector
        def _(dve):
            dve.wait_ge(idx_in, 16 * 5)
            dve.wait_ge(lut_in, 16)
            dve.tensor_copy(idxf[:, p_cols], idx[:, p_cols]).then_inc(idxf_done, 1)
            dve.tensor_copy(idxf[:, v_cols], idx[:, v_cols]).then_inc(idxf_done, 1)
            dve.memset(w_nat[:, v_cols], 0.0).then_inc(accv, 1)
            dve.wait_ge(idxf_done, 2)
            for k in range(LUT):
                dve.wait_ge(accv, k + 1)
                dve.tensor_scalar(eq_v[:, :], idxf[:, v_cols], float(k), None, ALU.is_equal).then_inc(eqv, 1)
                dve.wait_ge(eqv, k + 1)
                dve.scalar_tensor_tensor(w_nat[:, v_cols], eq_v[:, :], lut[:, k:k + 1], w_nat[:, v_cols],
                                         ALU.mult, ALU.add).then_inc(accv, 1)
            dve.wait_ge(split_hi, 2)
            dve.tensor_tensor(T["wout"][:, 1, :, :], wout_raw[:, :, :], T["wout"][:, 0, :, :].bitcast(F32),
                              ALU.subtract).then_inc(split_lo, 1)
            for n, (src, hi, lo) in enumerate(evacs):
                dve.wait_ge(tp_hi, n + 1)
                dve.tensor_tensor(lo, src, hi.bitcast(F32), ALU.subtract).then_inc(tp_lo, 1)

        @block.scalar
        def _(act):
            act.wait_ge(win_in, 16)
            act.wait_ge(zeroed, 4)
            act.activation(T["win"][:, 0, :, :, :].rearrange("p k c n -> p k (c n)")[:, :, 0:PROJ],
                           win_raw[:, :, :], ACT.Copy).then_inc(split_hi, 1)
            act.wait_ge(wout_in, 16)
            act.wait_ge(nw_in, 16 * (5 + HG))
            for k in range(4):
                act.activation(wout_raw[:, k, :], wout_raw[:, k, :], ACT.Copy,
                               scale=T["norm_w"][:, k:k + 1]).then_inc(wout_s, 1)
            act.wait_ge(wout_s, 4)
            act.activation(T["wout"][:, 0, :, :], wout_raw[:, :, :], ACT.Copy).then_inc(split_hi, 1)
            for n, (src, hi, lo) in enumerate(evacs):
                act.wait_ge(tp_done, n + 1)
                act.activation(hi, src, ACT.Copy).then_inc(tp_hi, 1)

        @block.tensor
        def _(pe):
            pe.wait_ge(ident_ok, 2)
            pe.wait_ge(accv, LUT + 1)
            pe.wait_ge(accp, LUT + 1)
            for n, job in enumerate(jobs):
                if n >= 8:
                    pe.wait_ge(tp_lo, n - 7)
                for out, src in job:
                    last = pe.transpose(out, src, T["ident"][:, :])
                last.then_inc(tp_done, 1)


class Norm:

    def __init__(self, nc, ctx, T, tag):
        sb = lambda n, s, d=F32: ctx.enter_context(nc.sbuf_tensor(tag + n, s, d))
        sem = lambda n: ctx.enter_context(nc.semaphore(tag + n))
        self.T = T
        self.stats = sb("stats", [P, GT, 6])
        self.mv = sb("mv", [P, GT, 2])
        self.ve = sb("ve", [P, GT])
        self.rstd = sb("rstd", [P, GT])
        self.xn = sb("xn", [P, GT, HID])
        self.xT = [sb(f"xT{b}", [P, 2, KC, GN], F32R) for b in range(2)]
        self.pt = ctx.enter_context(nc.psum_tensor(tag + "pt", [P, KC, GN], F32))
        self.stat_seen = sem("stat_seen")
        self.stat_ok, self.mv_ok, self.ve_ok, self.rstd_ok = map(sem, ("stat_ok", "mv_ok", "ve_ok", "rstd_ok"))
        self.xn_ok, self.pt_ok, self.hi_ok, self.lo_ok = map(sem, ("xn_ok", "pt_ok", "hi_ok", "lo_ok"))

    def dve_norm(self, dve, g):
        x = self.T["x_res"][:, :, :].rearrange("p t c -> p (t c)")
        for t in range(GT):
            dve.bn_stats(self.stats[:, t, :], x[:, bass.ds(g * (GT * HID) + t * HID, HID)]).then_inc(self.stat_ok, 1)
        dve.wait_ge(self.stat_ok, g * GT + GT)
        dve.sem_inc(self.stat_seen, 1)
        for t in range(GT):
            dve.bn_aggr(self.mv[:, t, :], self.stats[:, t, :]).then_inc(self.mv_ok, 1)
        dve.wait_ge(self.mv_ok, g * GT + GT)
        dve.tensor_scalar(self.ve[:, :], self.mv[:, :, 1], EPS, None, ALU.add).then_inc(self.ve_ok, 1)
        dve.wait_ge(self.rstd_ok, g + 1)
        dve.wait_ge(self.pt_ok, g + 1)
        for t in range(GT):
            dve.tensor_scalar(self.xn[:, t, :], x[:, bass.ds(g * (GT * HID) + t * HID, HID)],
                              self.mv[:, t, 0:1], self.rstd[:, t:t + 1],
                              ALU.subtract, ALU.mult).then_inc(self.xn_ok, 1)

    def pool_rstd(self, pool, g):
        pool.wait_ge(self.ve_ok, g + 1)
        pool.tensor_tensor(self.rstd[:, :], self.ve[:, :], self.T["m_half"][:, 0:GT], ALU.pow).then_inc(self.rstd_ok, 1)

    def pe_transpose(self, pe, g):
        pe.wait_ge(self.xn_ok, g * GT + GT)
        pe.wait_ge(self.lo_ok, g + 1)
        for kc in range(KC):
            for t in range(GT):
                last = pe.transpose(self.pt[:, kc, P * t:P * t + P], self.xn[:, t, P * kc:P * kc + P],
                                    self.T["ident"][:, :])
        last.then_inc(self.pt_ok, 1)

    def act_hi(self, act, g, par):
        act.wait_ge(self.pt_ok, g + 2)
        act.activation(self.xT[par][:, 0, :, :], self.pt[:, :, :], ACT.Copy).then_inc(self.hi_ok, 1)

    def dve_lo(self, dve, g, par):
        dve.wait_ge(self.hi_ok, g + 1)
        dve.tensor_tensor(self.xT[par][:, 1, :, :], self.pt[:, :, :], self.xT[par][:, 0, :, :].bitcast(F32),
                          ALU.subtract).then_inc(self.lo_ok, 1)

    def pe_ready(self, pe, g):
        pe.wait_ge(self.lo_ok, g + 2)


def build_ffn(nc, T, tag, out=None):
    with ExitStack() as ctx:
        sb = lambda n, s, d=F32: ctx.enter_context(nc.sbuf_tensor(tag + n, s, d))
        ps = lambda n, s: ctx.enter_context(nc.psum_tensor(tag + n, s, F32))
        sem = lambda n: ctx.enter_context(nc.semaphore(tag + n))
        norm = Norm(nc, ctx, T, tag)
        hT = sb("hT", [P, 2, FCH, GN], F32R)
        sg = [sb(f"sg{b}", [P, GN]) for b in range(2)]
        h = sb("h", [P, GN])
        gate = [ps(f"gate{b}", [P, GN]) for b in range(2)]
        up = [ps(f"up{b}", [P, GN]) for b in range(2)]
        down = ps("down", [P, GT, HID])
        gate_ok, up_ok, silu_ok, h_ok, h_hi, h_lo = map(sem, ("gate_ok", "up_ok", "silu_ok", "h_ok", "h_hi", "h_lo"))
        down_ok, res_ok, hz, stored = map(sem, ("down_ok", "res_ok", "hz", "stored"))
        wgu, wd, x_res = T["wgu"], T["wd"], T["x_res"]
        xflat = x_res[:, :, :].rearrange("p t c -> p (t c)")
        block = ctx.enter_context(nc.Block())

        def rows(c):
            return P if c < FCH - 1 else FLAST

        @block.vector
        def _(dve):
            dve.sem_inc(h_ok, 2)
            dve.sem_inc(norm.lo_ok, 1)
            with dve.Fori(0, GROUPS // 2) as i:
                for par in range(2):
                    g = i * 2 + par
                    norm.dve_norm(dve, g)
                    norm.dve_lo(dve, g, par)
                    for c in range(FCH):
                        r = rows(c)
                        dve.wait_ge(silu_ok, g * FCH + c + 1)
                        if c < FCH - 1:
                            dve.wait_ge(up_ok, g * (FCH - 1) + c + 1)
                            other = up[c % 2][:, :]
                        else:
                            other = gate[c % 2][64:64 + r, :]
                        dve.tensor_tensor(h[0:r, :], sg[c % 2][0:r, :], other, ALU.mult).then_inc(h_ok, 1)
                        dve.wait_ge(h_hi, g * FCH + c + 1)
                        dve.tensor_tensor(hT[0:r, 1, c, :], h[0:r, :], hT[0:r, 0, c, :].bitcast(F32),
                                          ALU.subtract).then_inc(h_lo, 1)
                        dve.wait_ge(h_lo, g * FCH + c + 1)
                    for t in range(0, GT, 2):
                        dve.wait_ge(down_ok, g * (GT // 2) + t // 2 + 1)
                        xt = xflat[:, bass.ds(g * (GT * HID) + t * HID, 2 * HID)]
                        dve.scalar_tensor_tensor(xt, down[:, t:t + 2, :].rearrange("p t c -> p (t c)"), 0.5, xt,
                                                 ALU.mult, ALU.add).then_inc(res_ok, 1)

        @block.gpsimd
        def _(pool):
            pool.memset(hT[:, 0, FCH - 1, :].bitcast(F32), 0.0).then_inc(hz, 1)
            pool.memset(hT[:, 1, FCH - 1, :].bitcast(F32), 0.0).then_inc(hz, 1)
            with pool.Fori(0, GROUPS) as g:
                norm.pool_rstd(pool, g)

        @block.scalar
        def _(act):
            act.wait_ge(hz, 2)
            with act.Fori(0, GROUPS // 2) as i:
                for par in range(2):
                    g = i * 2 + par
                    norm.act_hi(act, g, par)
                    for c in range(FCH):
                        r = rows(c)
                        act.wait_ge(gate_ok, g * FCH + c + 1)
                        act.activation(sg[c % 2][0:r, :], gate[c % 2][0:r, :], ACT.Silu).then_inc(silu_ok, 1)
                        act.wait_ge(h_ok, g * FCH + c + 3)
                        act.activation(hT[0:r, 0, c, :], h[0:r, :], ACT.Copy).then_inc(h_hi, 1)

        @block.tensor
        def _(pe):
            pe.sem_inc(norm.pt_ok, 1)
            pe.sem_inc(res_ok, GT // 2)
            pe.wait_ge(hz, 2)
            with pe.Fori(0, GROUPS // 2) as i:
                for par in range(2):
                    g = i * 2 + par
                    norm.pe_transpose(pe, g)
                    norm.pe_ready(pe, g)
                    x_hi, x_lo = norm.xT[par][:, 0], norm.xT[par][:, 1]
                    for c in range(FCH):
                        pe.wait_ge(h_ok, g * FCH + c + 1)
                        parts = [(gate[c % 2], c, gate_ok), (up[c % 2], 5 + c, up_ok)] if c < FCH - 1 \
                            else [(gate[c % 2], 10, gate_ok)]
                        for bank, wc, done in parts:
                            for kc in range(KC):
                                last = split_mm(pe, bank[:, :], wgu[:, 0, kc, wc, :], wgu[:, 1, kc, wc, :],
                                                x_hi[:, kc, :], x_lo[:, kc, :], kc == 0, kc == KC - 1)
                            last.then_inc(done, 1)
                    for t in range(GT):
                        if t == 0:
                            pe.wait_ge(h_lo, g * FCH + FCH)
                            pe.wait_ge(res_ok, g * (GT // 2) + GT // 2)
                        for c in range(FCH):
                            last = split_mm(pe, down[:, t, :], hT[:, 0, c, P * t:P * t + P],
                                            hT[:, 1, c, P * t:P * t + P], wd[:, 0, c, :], wd[:, 1, c, :],
                                            c == 0, c == FCH - 1)
                        if t % 2:
                            last.then_inc(down_ok, 1)

        if out is not None:
            @block.sync
            def _(sp):
                dst = out[0].rearrange("(t p) c -> p t c", p=P)
                for g in range(GROUPS):
                    sp.wait_ge(res_ok, (g + 2) * (GT // 2))
                    sp.dma_start(dst[:, g * GT:g * GT + GT, :], x_res[:, g * GT:g * GT + GT, :]).then_inc(stored, 16)
                sp.wait_ge(stored, 16 * GROUPS)


def build_in_proj(nc, T):
    with ExitStack() as ctx:
        sb = lambda n, s, d=F32: ctx.enter_context(nc.sbuf_tensor(n, s, d))
        sem = lambda n: ctx.enter_context(nc.semaphore(n))
        norm = Norm(nc, ctx, T, "m_")
        pre = [sb(f"pre{b}", [P, XCH, KCONV - 1 + GN]) for b in range(2)]
        bank = [ctx.enter_context(nc.psum_tensor(f"pj{b}", [P, GN], F32)) for b in range(4)]
        mm_ok, ev_ok, carry = map(sem, ("mm_ok", "ev_ok", "carry"))
        tap_v, w_ok = map(sem, ("tap_v", "w_ok"))
        win, cv, zs = T["win"], T["cv"], T["zs"]
        cw, cb = T["conv_w"], T["conv_b"]
        HALO = KCONV - 1
        block = ctx.enter_context(nc.Block())

        def v_conv(dve, g, par):
            n = 0
            for c in range(XCH):
                dve.wait_ge(ev_ok, g * PCH + (4 + c) + 2)
                dst = cv[:, c, bass.ds(g * GN, GN)]
                dve.tensor_scalar(dst, pre[par][:, c, HALO:HALO + GN], cw[:, c, HALO:HALO + 1], cb[:, c:c + 1],
                                  ALU.mult, ALU.add).then_inc(tap_v, 1)
                n += 1
                for k in range(HALO):
                    dve.wait_ge(tap_v, g * (KCONV * XCH) + n)
                    dve.scalar_tensor_tensor(dst, pre[par][:, c, k:k + GN], cw[:, c, k:k + 1], dst,
                                             ALU.mult, ALU.add).then_inc(tap_v, 1)
                    n += 1

        @block.vector
        def _(dve):
            dve.tensor_scalar(cw[:, :, :], cw[:, :, :], MUP_X, None, ALU.mult).then_inc(w_ok, 1)
            dve.memset(pre[0][:, :, 0:HALO], 0.0).then_inc(carry, 1)
            dve.sem_inc(norm.lo_ok, 1)
            dve.wait_ge(w_ok, 1)
            with dve.Fori(0, GROUPS // 2) as i:
                for par in range(2):
                    g = i * 2 + par
                    norm.dve_norm(dve, g)
                    norm.dve_lo(dve, g, par)
                    dve.wait_ge(carry, g + 1)
                    v_conv(dve, g, par)
                    dve.wait_ge(ev_ok, g * PCH + 4 + XCH + 1)
                    dve.tensor_copy(pre[1 - par][:, :, 0:HALO], pre[par][:, :, GN:GN + HALO]).then_inc(carry, 1)

        @block.gpsimd
        def _(pool):
            with pool.Fori(0, GROUPS) as g:
                norm.pool_rstd(pool, g)

        @block.scalar
        def _(act):
            act.sem_inc(ev_ok, 1)
            with act.Fori(0, GROUPS // 2) as i:
                for par in range(2):
                    g = i * 2 + par
                    norm.act_hi(act, g, par)
                    for c in range(PCH):
                        act.wait_ge(mm_ok, g * PCH + c + 1)
                        src = bank[c % 4]
                        if c < 4:
                            act.activation(zs[:, c, bass.ds(g * GN, GN)], src[:, :], ACT.Silu,
                                           scale=MUP_Z).then_inc(ev_ok, 1)
                        elif c < 4 + XCH:
                            if c == 4:
                                act.wait_ge(carry, g + 1)
                            act.activation(pre[par][:, c - 4, HALO:HALO + GN], src[:, :], ACT.Copy).then_inc(ev_ok, 1)
                        else:
                            act.activation(T["dt_raw"][:, bass.ds(g * GN, GN)], src[0:HEADS, :], ACT.Identity,
                                           bias=T["dt_b"][:, 0:1]).then_inc(ev_ok, 1)

        @block.tensor
        def _(pe):
            pe.sem_inc(norm.pt_ok, 1)
            with pe.Fori(0, GROUPS // 2) as i:
                for par in range(2):
                    g = i * 2 + par
                    norm.pe_transpose(pe, g)
                    norm.pe_ready(pe, g)
                    x_hi, x_lo = norm.xT[par][:, 0], norm.xT[par][:, 1]
                    for c in range(PCH):
                        pe.wait_ge(ev_ok, g * PCH + max(c - 3, 0) + 1)
                        for kc in range(KC):
                            last = split_mm(pe, bank[c % 4][:, :], win[:, 0, kc, c, :], win[:, 1, kc, c, :],
                                            x_hi[:, kc, :], x_lo[:, kc, :], kc == 0, kc == KC - 1)
                        last.then_inc(mm_ok, 1)


def build_decay(nc, T):
    with ExitStack() as ctx:
        sb = lambda n, s, d=F32: ctx.enter_context(nc.sbuf_tensor(n, s, d))
        sem = lambda n: ctx.enter_context(nc.semaphore(n))
        x = T["dt_raw"]
        t0, t1, t2, dt, a, a0, cp = (sb(n, [HEADS, L]) for n in ("t0", "t1", "t2", "dtT", "aT", "a0T", "cpT"))
        A = sb("A_neg", [HEADS, 1])
        eA = sb("eA", [HEADS, 1])
        dend = sb("dend", [HEADS, BLOCKS])
        dendT = sb("dendT", [BLOCKS, HEADS])
        pt_dt = ctx.enter_context(nc.psum_tensor("pt_dt", [P, TILES, HEADS], F32))
        pt_cp = ctx.enter_context(nc.psum_tensor("pt_cp", [P, TILES, HEADS], F32))
        pt_d = ctx.enter_context(nc.psum_tensor("pt_d", [BLOCKS, HEADS], F32))
        v_ok, s_ok, p_ok, z_ok, dma_ok = map(sem, ("v_ok", "s_ok", "p_ok", "z_ok", "dma_ok"))
        block = ctx.enter_context(nc.Block())
        V = dict(u=1, um1=2, r=3, d=4, dr=5, s=6, dt=7, A=8, a0=9, az=10, cp=11, dend=12, dT=13)
        S = dict(absx=1, e=2, ln=3, eA=4, a=5)

        @block.vector
        def _(dve):
            dve.wait_ge(s_ok, S["e"])
            dve.tensor_scalar(t1[:, :], t0[:, :], 1.0, None, ALU.add).then_inc(v_ok, 1)
            dve.wait_ge(v_ok, V["u"])
            dve.tensor_scalar(t2[:, :], t1[:, :], 1.0, None, ALU.subtract).then_inc(v_ok, 1)
            dve.reciprocal(a[:, :], t1[:, :]).then_inc(v_ok, 1)
            dve.wait_ge(v_ok, V["um1"])
            dve.tensor_tensor(t0[:, :], t0[:, :], t2[:, :], ALU.subtract).then_inc(v_ok, 1)
            dve.wait_ge(v_ok, V["d"])
            dve.tensor_tensor(t0[:, :], t0[:, :], a[:, :], ALU.mult).then_inc(v_ok, 1)
            dve.wait_ge(v_ok, V["dr"])
            dve.wait_ge(s_ok, S["ln"])
            dve.tensor_tensor(t0[:, :], t0[:, :], a0[:, :], ALU.add).then_inc(v_ok, 1)
            dve.wait_ge(v_ok, V["s"])
            dve.scalar_tensor_tensor(dt[:, :], x[:, :], 0.0, t0[:, :], ALU.max, ALU.add).then_inc(v_ok, 1)
            dve.wait_ge(s_ok, S["eA"])
            dve.tensor_scalar(A[:, :], eA[:, :], -1.0, None, ALU.mult).then_inc(v_ok, 1)
            dve.wait_ge(s_ok, S["a"])
            dve.wait_ge(z_ok, 1)
            dve.tensor_copy(t2[:, 0:L:Q], a[:, 0:L:Q]).then_inc(v_ok, 1)
            dve.wait_ge(v_ok, V["a0"])
            dve.memset(a[:, 0:L:Q], 0.0).then_inc(v_ok, 1)
            dve.wait_ge(v_ok, V["az"])
            dve.tensor_tensor_scan(cp[:, :], a[:, :], t2[:, :], 0.0, ALU.mult, ALU.add).then_inc(v_ok, 1)
            dve.wait_ge(v_ok, V["cp"])
            dve.tensor_copy(dend[:, :], cp[:, Q - 1:L:Q]).then_inc(v_ok, 1)
            dve.wait_ge(p_ok, 1)
            dve.tensor_copy(dendT[:, :], pt_d[:, :]).then_inc(v_ok, 1)
            dve.wait_ge(p_ok, 2)
            dve.tensor_copy(T["dt_tok"][:, :, :], pt_dt[:, :, :]).then_inc(v_ok, 1)
            dve.wait_ge(p_ok, 3)
            for b in range(NB):
                for q in range(4):
                    dve.tensor_copy(T["cp_g"][Q * q:Q * q + Q, :, b, :],
                                    pt_cp[Q * b:Q * b + Q, :, HG * q:HG * q + HG])

        @block.scalar
        def _(act):
            act.activation(t0[:, :], x[:, :], ACT.Abs).then_inc(s_ok, 1)
            act.wait_ge(s_ok, S["absx"])
            act.activation(t0[:, :], t0[:, :], ACT.Exp, scale=-1.0).then_inc(s_ok, 1)
            act.wait_ge(v_ok, V["u"])
            act.activation(a0[:, :], t1[:, :], ACT.Ln).then_inc(s_ok, 1)
            act.activation(eA[:, :], T["a_log"][:, :], ACT.Exp).then_inc(s_ok, 1)
            act.wait_ge(v_ok, V["A"])
            act.activation(a[:, :], dt[:, :], ACT.Exp, scale=A[:, 0:1]).then_inc(s_ok, 1)

        @block.gpsimd
        def _(pool):
            pool.wait_ge(v_ok, V["d"])
            pool.memset(t2[:, :], 0.0).then_inc(z_ok, 1)

        @block.tensor
        def _(pe):
            pe.wait_ge(v_ok, V["dend"])
            pe.transpose(pt_d[:, :], dend[:, :], T["ident"][0:HEADS, 0:HEADS]).then_inc(p_ok, 1)
            for src, dst in ((dt, pt_dt), (cp, pt_cp)):
                for t in range(TILES):
                    last = pe.transpose(dst[:, t, :], src[:, P * t:P * t + P], T["ident"][0:HEADS, 0:HEADS])
                last.then_inc(p_ok, 1)

        @block.sync
        def _(sp):
            sp.wait_ge(v_ok, V["az"])
            sp.dma_start(T["a_dram"].rearrange("b h i -> h b i"),
                         a[:, :].rearrange("h (b i) -> h b i", i=Q)).then_inc(dma_ok, 16)
            sp.wait_ge(v_ok, V["dT"])
            sp.dma_start(T["dend_dram"], dendT[:, :]).then_inc(dma_ok, 16)
            sp.wait_ge(dma_ok, 32)


def build_scan(nc, T):
    with ExitStack() as ctx:
        sb = lambda n, s, d=F32: ctx.enter_context(nc.sbuf_tensor(n, s, d))
        ps = lambda n, s: ctx.enter_context(nc.psum_tensor(n, s, F32))
        sem = lambda n: ctx.enter_context(nc.semaphore(n))
        HI = HEADS * Q
        d0 = [sb(f"d0_{b}", [P, HI]) for b in range(2)]
        dend = [sb(f"dend_{b}", [P, NB, HEADS]) for b in range(2)]
        eye_q = sb("eye_q", [P, HG * Q])
        lmat = sb("lmat", [P, HEADS, Q])
        mmat = sb("mmat", [P, HEADS, Q])
        xbd = sb("xbd", [P, HEADS, NB, PD])
        xT = [sb(f"xs_{b}", [P, 4, P]) for b in range(4)]
        bc = [sb(f"bc_{b}", [P, 2, P]) for b in range(2)]
        xdt, xr, tmp, yi, y, yf, sq, u = (sb(n, [P, INTER]) for n in ("xdt", "xr", "tmp", "yi", "y", "yf", "sq", "u"))
        bm = sb("bm", [P, NB, NS])
        gs = [sb(f"gs_{b}", [P, Q]) for b in range(2)]
        s0 = [sb(f"s0_{b}", [P, INTER]) for b in range(2)]
        s123 = sb("s123", [P, NB - 1, INTER])
        ssum = sb("ssum", [P, P])
        ve = sb("ve_y", [P, 1])
        rstd = sb("rstd_y", [P, 1])
        uh = sb("uh", [P, 2, 4, P], F32R)
        X, BG = ps("X", [P, INTER]), ps("BG", [P, NS + Q + 1])
        new = [ps(f"new{b}", [P, INTER]) for b in range(2)]
        intra, yint = ps("intra", [P, NB, HG, PD]), ps("yint", [P, NB, HG * PD])
        ytr, outp = ps("ytr", [P, NB, P]), ps("outp", [P, HID])
        names = ("scan_ok", "smul_ok", "xs_ok", "bc_ok", "tr_ok", "gs_ok", "bm_ok", "xdt_ok", "xbd_ok", "xr_ok",
                 "m_ok", "new_ok", "add_ok", "yint_ok", "intra_ok", "yi_ok", "y_ok", "ytr_ok", "yf_ok", "sq_ok",
                 "u_ok", "uhi_ok", "ulo_ok", "red_ok", "ss_ok", "ve_ok", "rs_ok", "out_ok", "res_ok", "set_ok",
                 "eye_ok")
        s = {n: sem("c_" + n) for n in names}
        d0_in = [sem(f"d0_in{b}") for b in range(2)]
        dend_in = [sem(f"dend_in{b}") for b in range(2)]
        FREE = dict(scan_ok=2, smul_ok=8, m_ok=2, yint_ok=2, new_ok=4, intra_ok=1, xdt_ok=1, bm_ok=4, gs_ok=1,
                    add_ok=2, y_ok=1, yf_ok=16, res_ok=1, xbd_ok=4, ytr_ok=1, sq_ok=1, uhi_ok=1, ss_ok=1,
                    out_ok=1, u_ok=1, ulo_ok=1, red_ok=1, ve_ok=2)
        PER = dict(smul_ok=4, new_ok=4, bm_ok=4, add_ok=4, xbd_ok=4, yf_ok=4)
        cv, zs, x_res, wout = T["cv"], T["zs"], T["x_res"], T["wout"]
        block = ctx.enter_context(nc.Block())

        def times(tile, mul):
            i, c = tile
            return c * mul if i is None else i * (4 * mul) + c * mul

        def count(name, tile, after=0, part=0):
            i, c = tile
            per = PER.get(name, 1)
            base = FREE.get(name, 0) + (part if part else per)
            return times((i, c + after), per) + base

        def wait(eng, name, tile, after=0, part=0):
            value = count(name, tile, after, part)
            if tile[0] is not None or value > 0:
                eng.wait_ge(s[name], value)

        def half(tile):
            i, c = tile
            return c // 2 + 1 if i is None else i * 2 + c // 2 + 1

        def pipeline(eng, step):
            for t in range(2):
                step(t, None, True, t >= 1, False)
            with eng.Fori(0, (TILES - 4) // 4) as i:
                for k in range(4):
                    step(2 + k, i, True, True, True)
            for t in range(TILES - 2, TILES + 2):
                step(t, None, t < TILES, t - 1 < TILES, True)

        @block.sync
        def _(sp):
            with sp.Fori(0, TILES // 4) as i:
                for c in range(4):
                    tile = (i, c)
                    wait(sp, "scan_ok", tile, -2)
                    for b in range(NB):
                        src = T["a_dram"].rearrange("b h i -> b (h i)")[bass.ds(i * 16 + c * 4 + b, 1), :]
                        sp.dma_start(d0[c % 2][Q * b:Q * b + Q, :], src.broadcast_to([Q, HI])).then_inc(d0_in[c % 2], 16)
                    wait(sp, "smul_ok", tile, -2)
                    src = T["dend_dram"].rearrange("(t b) h -> t (b h)", b=NB)[bass.ds(i * 4 + c, 1), :]
                    sp.dma_start(dend[c % 2][:, :, :].rearrange("p b h -> p (b h)"),
                                 src.broadcast_to([P, NB * HEADS])).then_inc(dend_in[c % 2], 16)

        @block.scalar
        def _(act):
            act.sem_inc(s["bm_ok"], FREE["bm_ok"])
            act.sem_inc(s["gs_ok"], FREE["gs_ok"])
            act.sem_inc(s["xbd_ok"], FREE["xbd_ok"])
            act.sem_inc(s["sq_ok"], FREE["sq_ok"])
            act.sem_inc(s["uhi_ok"], FREE["uhi_ok"])
            act.wait_ge(s["set_ok"], 2)

            def step(c, i, do_a, do_b, do_c):
                a, z = (i, c), (i, c - 2)
                if do_a:
                    tok = bass.ds(times(a, P), P)
                    wait(act, "yf_ok", a, -4)
                    act.activation(xT[c % 4][:, :, :], cv[:, 0:4, tok], ACT.Silu).then_inc(s["xs_ok"], 1)
                    wait(act, "yint_ok", a, -2)
                    act.activation(bc[c % 2][:, :, :], cv[:, 4:6, tok], ACT.Silu).then_inc(s["bc_ok"], 1)
                if do_c:
                    wait(act, "yf_ok", z)
                    wait(act, "red_ok", z, -1)
                    act.activation(sq[:, :], yf[:, :], ACT.Square).then_inc(s["sq_ok"], 1)
                    wait(act, "u_ok", z)
                    wait(act, "out_ok", z, -1)
                    act.activation(uh[:, 0, :, :], u[:, :].rearrange("p (g t) -> p g t", g=4), ACT.Copy
                                   ).then_inc(s["uhi_ok"], 1)
                if do_a:
                    wait(act, "tr_ok", a)
                    wait(act, "m_ok", a, -2)
                    act.activation(gs[c % 2][:, :], BG[:, NS:NS + Q], ACT.Copy).then_inc(s["gs_ok"], 1)
                    wait(act, "new_ok", a, -1)
                    for b in range(NB):
                        r = slice(Q * b, Q * b + Q)
                        act.activation(bm[r, b, :], BG[r, 0:NS], ACT.Copy).then_inc(s["bm_ok"], 1)
                    wait(act, "xdt_ok", a)
                    wait(act, "intra_ok", a, -1)
                    for b in range(NB):
                        r = slice(Q * b, Q * b + Q)
                        act.activation(xbd[r, :, b, :], xdt[r, :].rearrange("p (h d) -> p h d", d=PD), ACT.Copy
                                       ).then_inc(s["xbd_ok"], 1)

            pipeline(act, step)

        @block.vector
        def _(dve):
            for n in ("scan_ok", "xdt_ok", "y_ok", "yf_ok", "res_ok", "u_ok", "ulo_ok", "red_ok", "ve_ok"):
                dve.sem_inc(s[n], FREE[n])
            dve.memset(s0[0][:, :], 0.0).then_inc(s["add_ok"], FREE["add_ok"])
            dve.wait_ge(s["eye_ok"], 2)

            def step(c, i, do_a, do_b, do_c):
                a, b_, z = (i, c), (i, c - 1), (i, c - 2)
                if do_c:
                    wait(dve, "ytr_ok", z)
                    wait(dve, "sq_ok", z, -1)
                    wait(dve, "u_ok", z, -1)
                    for g in range(4):
                        dve.scalar_tensor_tensor(
                            yf[:, P * g:P * g + P].rearrange("p (b t) -> p b t", b=NB),
                            xT[(c - 2) % 4][:, g, :].rearrange("p (b t) -> p b t", b=NB), T["d_ch"][:, g:g + 1],
                            ytr[:, :, Q * g:Q * g + Q], ALU.mult, ALU.add).then_inc(s["yf_ok"], 1)
                    wait(dve, "yf_ok", z)
                    wait(dve, "uhi_ok", z, -1)
                    wait(dve, "ulo_ok", z, -1)
                    dve.tensor_tensor(u[:, :].rearrange("p (g t) -> p g t", g=4),
                                      yf[:, :].rearrange("p (g t) -> p g t", g=4),
                                      zs[:, :, bass.ds(times(z, P), P)], ALU.mult).then_inc(s["u_ok"], 1)
                    wait(dve, "sq_ok", z)
                    wait(dve, "ss_ok", z, -1)
                    dve.tensor_reduce(ssum[:, :], sq[:, :].rearrange("p (g t) -> p t g", g=4),
                                      mybir.AxisListType.X, ALU.add).then_inc(s["red_ok"], 1)
                    wait(dve, "uhi_ok", z)
                    dve.tensor_tensor(uh[:, 1, :, :].rearrange("p g t -> p (g t)"), u[:, :],
                                      uh[:, 0, :, :].bitcast(F32).rearrange("p g t -> p (g t)"), ALU.subtract
                                      ).then_inc(s["ulo_ok"], 1)
                if do_a:
                    wait(dve, "tr_ok", a)
                    wait(dve, "xbd_ok", a, -1)
                    wait(dve, "xr_ok", a, -1)
                    dt = T["dt_tok"][:, :, :].rearrange("p t h -> p (t h)")[:, bass.ds(times(a, HEADS), HEADS)]
                    dve.tensor_tensor(xdt[:, :].rearrange("p (h d) -> p h d", d=PD),
                                      X[:, :].rearrange("p (h d) -> p h d", d=PD),
                                      dt.unsqueeze(2).broadcast_to([P, HEADS, PD]), ALU.mult).then_inc(s["xdt_ok"], 1)
                    dve.wait_ge(d0_in[c % 2], half(a) * (16 * NB))
                    wait(dve, "m_ok", a, -1)
                    lflat = lmat[:, :, :].rearrange("p h i -> p (h i)")
                    for q in range(4):
                        cols = slice(HG * Q * q, HG * Q * (q + 1))
                        ins = dve.tensor_tensor_scan(lflat[:, cols], d0[c % 2][:, cols], eye_q[:, :], 0.0,
                                                     ALU.mult, ALU.add)
                    ins.then_inc(s["scan_ok"], 1)
                if do_b:
                    wait(dve, "yint_ok", b_, -1)
                    for b in range(NB):
                        wait(dve, "new_ok", b_, 0, b + 1)
                        wait(dve, "smul_ok", b_, 0, b + 1)
                        dst = s123[:, b, :] if b < NB - 1 else s0[c % 2][:, :]
                        dve.tensor_tensor(dst, tmp[:, :], new[b % 2][:, :], ALU.add).then_inc(s["add_ok"], 1)
                if do_a:
                    wait(dve, "xdt_ok", a)
                    wait(dve, "scan_ok", a)
                    wait(dve, "new_ok", a, -1)
                    dve.tensor_tensor(xr[:, :].rearrange("p (h d) -> p h d", d=PD),
                                      xdt[:, :].rearrange("p (h d) -> p h d", d=PD),
                                      lmat[:, :, Q - 1:Q].broadcast_to([P, HEADS, PD]), ALU.mult
                                      ).then_inc(s["xr_ok"], 1)
                if do_b:
                    wait(dve, "yint_ok", b_)
                    wait(dve, "y_ok", b_, -1)
                    cp = T["cp_g"][:, :, :, :].rearrange("p t b h -> p (t b h)")[:, bass.ds(times(b_, HEADS), HEADS)]
                    dve.tensor_tensor(yi[:, :].rearrange("p (h d) -> p h d", d=PD),
                                      yint[:, :, :].rearrange("p b (h d) -> p (b h) d", d=PD),
                                      cp.unsqueeze(2).broadcast_to([P, HEADS, PD]), ALU.mult).then_inc(s["yi_ok"], 1)
                    wait(dve, "yi_ok", b_)
                    wait(dve, "intra_ok", b_)
                    wait(dve, "ytr_ok", b_, -1)
                    dve.tensor_tensor(y[:, :], yi[:, :], intra[:, :, :, :].rearrange("p b h d -> p (b h d)"),
                                      ALU.add).then_inc(s["y_ok"], 1)
                if do_c:
                    wait(dve, "ss_ok", z)
                    dve.tensor_scalar(ve[:, :], BG[:, NS + Q:NS + Q + 1], 1.0 / INTER, EPS, ALU.mult, ALU.add
                                      ).then_inc(s["ve_ok"], 1)
                    wait(dve, "out_ok", z)
                    wait(dve, "rs_ok", z)
                    xt = x_res[:, :, :].rearrange("p t c -> p (t c)")[:, bass.ds(times(z, HID), HID)]
                    dve.scalar_tensor_tensor(xt, outp[:, :], rstd[:, 0:1], xt, ALU.mult, ALU.add
                                             ).then_inc(s["res_ok"], 1)

            pipeline(dve, step)

        @block.gpsimd
        def _(pool):
            pool.sem_inc(s["smul_ok"], FREE["smul_ok"])
            pool.sem_inc(s["m_ok"], FREE["m_ok"])
            pool.memset(xbd[:, :, :, :], 0.0).then_inc(s["set_ok"], 1)
            pool.memset(bm[:, :, :], 0.0).then_inc(s["set_ok"], 1)
            pool.memset(eye_q[:, :], 0.0).then_inc(s["eye_ok"], 1)
            pool.wait_ge(s["eye_ok"], 1)
            for b in range(NB):
                part = eye_q[Q * b:Q * b + Q, :].rearrange("p (h i) -> p h i", i=Q)
                ins = pool.affine_select(out=part, in_=part, compare_op=ALU.not_equal, fill=1.0, base=0,
                                         pattern=[[0, HG], [-1, Q]], channel_multiplier=1)
            ins.then_inc(s["eye_ok"], 1)

            def step(c, i, do_a, do_b, do_c):
                a, b_, z = (i, c), (i, c - 1), (i, c - 2)
                if do_b:
                    pool.wait_ge(dend_in[(c - 1) % 2], half(b_) * 16)
                    for b in range(NB):
                        wait(pool, "add_ok", b_, 0, b) if b else wait(pool, "add_ok", b_, -1)
                        src = s0[(c - 1) % 2][:, :] if b == 0 else s123[:, b - 1, :]
                        pool.tensor_tensor(tmp[:, :].rearrange("p (h d) -> p h d", d=PD),
                                           src.rearrange("p (h d) -> p h d", d=PD),
                                           dend[(c - 1) % 2][:, b, :].unsqueeze(2).broadcast_to([P, HEADS, PD]),
                                           ALU.mult).then_inc(s["smul_ok"], 1)
                if do_a:
                    wait(pool, "scan_ok", a)
                    wait(pool, "gs_ok", a)
                    wait(pool, "intra_ok", a, -1)
                    pool.tensor_tensor(mmat[:, :, :], lmat[:, :, :],
                                       gs[c % 2][:, :].unsqueeze(1).broadcast_to([P, HEADS, Q]), ALU.mult
                                       ).then_inc(s["m_ok"], 1)
                if do_c:
                    wait(pool, "ve_ok", z)
                    wait(pool, "res_ok", z, -1)
                    pool.tensor_tensor(rstd[:, :], ve[:, :], T["m_half"][:, 0:1], ALU.pow).then_inc(s["rs_ok"], 1)

            pipeline(pool, step)

        @block.tensor
        def _(pe):
            for n in ("yint_ok", "new_ok", "intra_ok", "ytr_ok", "ss_ok", "out_ok"):
                pe.sem_inc(s[n], FREE[n])

            def step(c, i, do_a, do_b, do_c):
                a, b_, z = (i, c), (i, c - 1), (i, c - 2)
                if do_c:
                    wait(pe, "y_ok", z)
                    wait(pe, "yf_ok", z, -1)
                    for b in range(NB):
                        ins = pe.transpose(ytr[:, b, :], y[:, P * b:P * b + P], T["ident"][:, :])
                    ins.then_inc(s["ytr_ok"], 1)
                if do_a:
                    wait(pe, "xs_ok", a)
                    wait(pe, "xdt_ok", a, -1)
                    for g in range(4):
                        pe.transpose(X[:, P * g:P * g + P], xT[c % 4][:, g, :], T["ident"][:, :])
                    wait(pe, "bc_ok", a)
                    wait(pe, "bm_ok", a, -1)
                    wait(pe, "gs_ok", a, -1)
                    wait(pe, "ve_ok", a, -3)
                    pe.transpose(BG[:, 0:NS], bc[c % 2][:, 0, :], T["ident"][:, :])
                    for b in range(NB):
                        r = slice(Q * b, Q * b + Q)
                        ins = pe.matmul(BG[r, NS:NS + Q], bc[c % 2][:, 0, r], bc[c % 2][:, 1, r], start=True, stop=True)
                    ins.then_inc(s["tr_ok"], 1)
                if do_b:
                    wait(pe, "xr_ok", b_)
                    wait(pe, "bm_ok", b_)
                    for b in range(NB):
                        pe.wait_ge(s["add_ok"], times(b_, NB) + b + 1)
                        pe.matmul(new[b % 2][:, :], bm[:, b, :], xr[:, :], start=True, stop=True
                                  ).then_inc(s["new_ok"], 1)
                    wait(pe, "m_ok", b_)
                    wait(pe, "xbd_ok", b_)
                    wait(pe, "y_ok", b_, -1)
                    for hh in range(HG):
                        for g in range(4):
                            h = HG * g + hh
                            ins = pe.matmul(intra[Q * g:Q * g + Q, :, hh, :], mmat[:, h, :], xbd[:, h, :, :],
                                            start=True, stop=True)
                    ins.then_inc(s["intra_ok"], 1)
                    for b in range(NB):
                        wait(pe, "add_ok", b_, 0, b) if b else wait(pe, "add_ok", b_, -1)
                        st = s0[(c - 1) % 2] if b == 0 else s123[:, b - 1, :]
                        for g in range(4):
                            ins = pe.matmul(yint[Q * g:Q * g + Q, b, :], bc[(c - 1) % 2][:, 1, Q * b:Q * b + Q],
                                            st[:, P * g:P * g + P], start=True, stop=True)
                    ins.then_inc(s["yint_ok"], 1)
                if do_c:
                    wait(pe, "red_ok", z)
                    if do_a:
                        wait(pe, "bm_ok", a)
                    pe.matmul(BG[:, NS + Q:NS + Q + 1], ssum[:, :], T["ones"][:, 0:1], start=True, stop=True
                              ).then_inc(s["ss_ok"], 1)
                    wait(pe, "ulo_ok", z)
                    wait(pe, "res_ok", z, -1)
                    for k in range(4):
                        ins = split_mm(pe, outp[:, :], uh[:, 0, k, :], uh[:, 1, k, :], wout[:, 0, k, :],
                                       wout[:, 1, k, :], k == 0, k == 3)
                    ins.then_inc(s["out_ok"], 1)

            pipeline(pe, step)


def move_weights(nc, T, tag, save):
    with ExitStack() as ctx:
        moved = ctx.enter_context(nc.semaphore(tag + "moved"))
        block = ctx.enter_context(nc.Block())

        @block.sync
        def _(sp):
            for name in ("wgu", "wd"):
                chip = T[name][tuple([slice(None)] * len(T[name].shape))].bitcast(F32)
                pair = (T[name + "_dram"], chip) if save else (chip, T[name + "_dram"])
                sp.dma_start(*pair).then_inc(moved, 16)
            sp.wait_ge(moved, 32)


def build(nc, A, out):
    T = {}
    for name, shape, dt in (("a_dram", (BLOCKS, HEADS, Q), F32), ("dend_dram", (BLOCKS, HEADS), F32),
                            ("wgu_dram", (P, 2, KC, GUC, P), F32), ("wd_dram", (P, 2, FCH, HID), F32)):
        T[name] = nc.dram_tensor(name, shape, dt, kind="Internal").ap()
    with ExitStack() as base:
        def put(stack, *tensors, side="left"):
            for name, shape, *dt in tensors:
                T[name] = stack.enter_context(nc.sbuf_tensor(f"{name}_{len(T)}", shape, (dt or [F32])[0], side=side))

        put(base, ("x_res", [P, TILES, HID]), ("wout", [P, 2, 4, HID], F32R), ("ident", [P, P]), ("ones", [P, 1]),
            ("m_half", [P, GT]), ("norm_w", [P, 4]), ("conv_b", [P, XCH]), ("conv_w", [P, XCH, KCONV]),
            ("a_log", [HEADS, 1]), ("dt_b", [HEADS, 1]), ("d_ch", [P, 4]))
        ffn_w = (("wgu", [P, 2, KC, GUC, P], F32R), ("wd", [P, 2, FCH, HID], F32R))
        with ExitStack() as win_s:
            put(win_s, ("win", [P, 2, KC, PCH, P], F32R), side="right")
            with ExitStack() as ffn1:
                put(ffn1, *ffn_w)
                build_weights(nc, T, A)
                build_ffn(nc, T, "f1_")
                move_weights(nc, T, "sv_", True)
            mamba = ExitStack()
            put(mamba, ("cv", [P, XCH, L]), ("zs", [P, 4, L]), ("dt_tok", [P, TILES, HEADS]),
                ("cp_g", [P, TILES, NB, HG]))
            raw = ExitStack()
            put(raw, ("dt_raw", [HEADS, L]))
            build_in_proj(nc, T)
        build_decay(nc, T)
        raw.close()
        build_scan(nc, T)
        mamba.close()
        with ExitStack() as ffn2:
            put(ffn2, *ffn_w)
            move_weights(nc, T, "ld_", False)
            build_ffn(nc, T, "f2_", out)


_INS = dict(x="L0_attn_hidden_states", in_w="L0_attn_in_proj_w", conv_w="L0_attn_conv_w", conv_b="L0_attn_conv_b",
            A_log="L0_attn_A_log", D="L0_attn_D", dt_bias="L0_attn_dt_bias", norm_w="L0_attn_norm_w",
            out_w="L0_attn_out_proj_w", lut="L0_ffn_lut", gate="L0_ffn_gate_idx", up="L0_ffn_up_idx",
            down="L0_ffn_down_idx")


def kernel(**inputs):
    import numpy as _np
    import concourse.bacc as _bacc
    from concourse.bass_utils import run_bass_kernel_spmd as _run

    nc = _bacc.Bacc("TRN2", target_bir_lowering=False, num_devices=1)
    arrays, args = {}, {}
    for short, name in _INS.items():
        a = _np.ascontiguousarray(inputs[name])
        arrays[f"in_{short}"] = a
        args[short] = nc.dram_tensor(f"in_{short}", a.shape, mybir.dt.from_np(a.dtype), kind="ExternalInput").ap()
    out = nc.dram_tensor("out_0", (1, L, HID), F32, kind="ExternalOutput").ap()
    build(nc, args, out)
    return _run(nc, [arrays], core_ids=[0]).results[0]["out_0"]
```

```python
from contextlib import ExitStack

import concourse.bass as bass
from concourse import mybir

F32 = mybir.dt.float32
F32R = mybir.dt.float32r
I32 = mybir.dt.int32
ALU = mybir.AluOpType
ACT = mybir.ActivationFunctionType

P = 128
L = 2048
HID = 256
KC = HID // P
TILES = L // P
GT = 4
GROUPS = TILES // GT
GN = GT * P
FF = 688
FCH = 6
FLAST = FF - 5 * P
LUT = 16
INTER = 512
HEADS = 64
PD = INTER // HEADS
NS = 128
KCONV = 4
CONV = INTER + 2 * NS
PROJ = 2 * INTER + 2 * NS + HEADS
PCH = 11
XCH = CONV // P
Q = 32
NB = P // Q
BLOCKS = L // Q
HG = 16
EPS = 1e-5
MUP_Z, MUP_X = 0.25, 0.5
GUC = 11


def split_mm(pe, out, w_hi, w_lo, x_hi, x_lo, start, stop):
    pe.matmul(out, w_hi, x_hi, start=start, stop=False)
    pe.matmul(out, w_hi, x_lo, start=False, stop=False)
    return pe.matmul(out, w_lo, x_hi, start=False, stop=stop)


def build_weights(nc, T, A, norm):
    with ExitStack() as ctx:
        sb = lambda n, s, d=F32: ctx.enter_context(nc.sbuf_tensor(n, s, d))
        sem = lambda n: ctx.enter_context(nc.semaphore(n))
        gu_idx = sb("gu_idx", [P, GUC, HID], I32)
        dn_idx = sb("dn_idx", [P, 2, FF], I32)
        mask = [sb(f"mask{b}", [P, LUT, HID], F32R) for b in range(2)]
        lut = sb("lut_bc", [P, LUT])
        lut_h, lut_l = sb("lut_h", [P, LUT], F32R), sb("lut_l", [P, LUT], F32R)
        diag = sb("diag", [P, LUT, 2, P], F32R)
        win_raw = sb("win_raw", [P, KC, PROJ])
        wout_raw = sb("wout_raw", [P, 4, HID])
        bank = [ctx.enter_context(nc.psum_tensor(f"look{b}", [P, 2, 2, P], F32)) for b in range(2)]
        idx_pad, gate_in, up_in, mix_in, down_in, lut_in, x_in, small_in, win_in, wout_in = map(sem, (
            "idx_pad", "gate_in", "up_in", "mix_in", "down_in", "lut_in", "x_in", "small_in", "win_in", "wout_in"))
        lut_ok, diag_ok, mask_ok, prod_ok, evac_ok, zeroed, split_hi, wout_s, split_lo, ident_ok = map(sem, (
            "lut_ok", "diag_ok", "mask_ok", "prod_ok", "evac_ok", "zeroed", "split_hi", "wout_s", "split_lo",
            "ident_ok"))
        win, wout, wgu, wd = T["win"], T["wout"], T["wgu"], T["wd"]
        DOWN = [(m, 2 * P * j, min(2 * P, FF - 2 * P * j), [(f, min(P, FF - P * f)) for f in (2 * j, 2 * j + 1)])
                for m in range(2) for j in range(FCH // 2)]
        x0_in, half_ok, *first_in = map(sem, ("x0_in", "half_ok", "first_in0", "first_in1"))
        x_in_dram = A["x"][0].rearrange("(t p) c -> p t c", p=P)
        block = ctx.enter_context(nc.Block())

        @block.sync
        def _(sp):
            sp.dma_start(lut[:, :], A["lut"].unsqueeze(0).broadcast_to([P, LUT])).then_inc(lut_in, 16)
            for c in range(2):
                sp.dma_start(gu_idx[:, c, :], A["gate"][c * P:c * P + P, :]).then_inc(first_in[c], 16)
            sp.dma_start(gu_idx[:, 2:5, :], A["gate"][2 * P:5 * P, :].rearrange("(c p) h -> p c h", p=P)
                         ).then_inc(gate_in, 16)
            sp.dma_start(T["x_res"][:, 0:GT, :], x_in_dram[:, 0:GT, :]).then_inc(x0_in, 16)
            sp.wait_ge(idx_pad, 1)
            sp.dma_start(gu_idx[0:FLAST, 10, :], A["gate"][5 * P:FF, :]).then_inc(mix_in, 16)
            sp.dma_start(gu_idx[64:64 + FLAST, 10, :], A["up"][5 * P:FF, :]).then_inc(mix_in, 16)
            sp.dma_start(dn_idx[:, :, :], A["down"].rearrange("(c p) f -> p c f", p=P)).then_inc(down_in, 16)
            sp.dma_start(win_raw[:, :, :], A["in_w"].rearrange("(k p) n -> p k n", p=P)).then_inc(win_in, 16)
            sp.dma_start(T["x_res"][:, GT:, :], x_in_dram[:, GT:, :]).then_inc(x_in, 16)
            sp.dma_start(wout_raw[:, :, :], A["out_w"].rearrange("(k p) n -> p k n", p=P)).then_inc(wout_in, 16)
            with nc.allow_non_contiguous_dma(reason="per-channel vectors, small"):
                sp.dma_start(T["norm_w"][:, :], A["norm_w"].rearrange("(k p) -> p k", p=P)).then_inc(small_in, 16)
                sp.dma_start(T["conv_b"][:, :], A["conv_b"].rearrange("(k p) -> p k", p=P)).then_inc(small_in, 16)
                sp.dma_start(T["conv_w"][:, :, :], A["conv_w"].rearrange("(k p) j -> p k j", p=P)
                             ).then_inc(small_in, 16)
                for half in range(2):
                    r = slice(HEADS * half, HEADS * half + HEADS)
                    sp.dma_start(T["a_log"][r, :], A["A_log"].unsqueeze(1)).then_inc(small_in, 16)
                    sp.dma_start(T["dt_b"][r, :], A["dt_bias"].unsqueeze(1)).then_inc(small_in, 16)
                for hh in range(HG):
                    sp.dma_start(T["d_ch"][PD * hh:PD * hh + PD, :],
                                 A["D"].rearrange("(g h) -> h g", h=HG)[hh:hh + 1, :].broadcast_to([PD, 4])
                                 ).then_inc(small_in, 16)
            sp.wait_ge(x_in, 16)
            sp.wait_ge(small_in, 16 * (7 + HG))

        @block.gpsimd
        def _(pool):
            pool.memset(T["ident"][:, :], 0.0).then_inc(ident_ok, 1)
            pool.wait_ge(ident_ok, 1)
            pool.affine_select(out=T["ident"][:, :], in_=T["ident"][:, :], compare_op=ALU.not_equal, fill=1.0,
                               base=0, pattern=[[-1, P]], channel_multiplier=1).then_inc(ident_ok, 1)
            pool.memset(gu_idx[:, GUC - 1, :], LUT).then_inc(idx_pad, 1)
            pool.memset(T["ones"][:, :], 1.0)
            pool.memset(T["m_half"][:, :], -0.5).then_inc(half_ok, 1)
            for hl in range(2):
                pool.memset(wd[:, hl, FCH - 1, :].bitcast(F32), 0.0).then_inc(zeroed, 1)
            pool.wait_ge(half_ok, 1)
            norm.pool_rstd(pool, 0)
            pool.wait_ge(split_hi, 2)
            pool.tensor_tensor(win[:, 1, :, :, :].rearrange("p k c n -> p k (c n)")[:, :, 0:PROJ], win_raw[:, :, :],
                               win[:, 0, :, :, :].rearrange("p k c n -> p k (c n)")[:, :, 0:PROJ].bitcast(F32),
                               ALU.subtract)
            pool.tensor_tensor(win[:, 1, :, PCH - 1, HEADS:P], win_raw[:, :, PROJ - HEADS:PROJ],
                               win[:, 0, :, PCH - 1, HEADS:P].bitcast(F32), ALU.subtract)
            pool.wait_ge(split_hi, 3)
            pool.tensor_tensor(wout[:, 1, :, :], wout_raw[:, :, :], wout[:, 0, :, :].bitcast(F32), ALU.subtract)

        @block.vector
        def _(dve):
            dve.wait_ge(lut_in, 16)
            dve.tensor_copy(lut_h[:, :], lut[:, :]).then_inc(lut_ok, 1)
            dve.wait_ge(lut_ok, 1)
            dve.tensor_tensor(lut_l[:, :], lut[:, :], lut_h[:, :].bitcast(F32), ALU.subtract).then_inc(lut_ok, 1)
            dve.wait_ge(lut_ok, 2)
            dve.wait_ge(ident_ok, 2)
            for k in range(LUT):
                for hl, part in enumerate((lut_h, lut_l)):
                    dve.tensor_scalar(diag[:, k, hl, :], T["ident"][:, :], part[:, k:k + 1].bitcast(F32), None,
                                      ALU.mult).then_inc(diag_ok, 1)

            def masks(b, src, n, unit):
                dve.wait_ge(prod_ok, unit + 1)
                for k in range(LUT):
                    dve.tensor_scalar(mask[b][:, k, 0:n], src, float(k), None, ALU.is_equal).then_inc(mask_ok, 1)

            dve.sem_inc(prod_ok, 2)
            gu = gu_idx[:, :, :].rearrange("p c h -> p (c h)")
            for unit in range(2):
                dve.wait_ge(first_in[unit], 16)
                masks(unit, gu_idx[:, unit, :], HID, unit)
            dve.wait_ge(gate_in, 16)
            dve.wait_ge(up_in, 16)
            dve.wait_ge(x0_in, 16)
            norm.dve_start(dve)
            norm.dve_stats(dve, 0)
            norm.dve_xn(dve, 0)
            with dve.Fori(1, GUC // 2) as i:
                for b in range(2):
                    masks(b, gu[:, bass.ds(i * (2 * HID) + b * HID, HID)], HID, i * 2 + b)
            dve.wait_ge(mix_in, 32)
            masks(0, gu_idx[:, GUC - 1, :], HID, GUC - 1)
            dve.wait_ge(down_in, 16)
            for n, (m, f0, cols, _) in enumerate(DOWN):
                masks((GUC + n) % 2, dn_idx[:, m, f0:f0 + cols], cols, GUC + n)
            norm.dve_lo(dve, 0)

        @block.scalar
        def _(act):
            act.dma_start(gu_idx[:, 5:10, :], A["up"][0:5 * P, :].rearrange("(c p) h -> p c h", p=P)
                          ).then_inc(up_in, 16)
            def win_hi():
                act.wait_ge(win_in, 16)
                act.activation(win[:, 0, :, :, :].rearrange("p k c n -> p k (c n)")[:, :, 0:PROJ], win_raw[:, :, :],
                               ACT.Copy).then_inc(split_hi, 1)
                act.activation(win[:, 0, :, PCH - 1, HEADS:P], win_raw[:, :, PROJ - HEADS:PROJ], ACT.Copy
                               ).then_inc(split_hi, 1)

            act.sem_inc(evac_ok, 2)

            def evac(b, unit, squares):
                act.wait_ge(prod_ok, unit + 3)
                for n, (dst, rows) in enumerate(squares):
                    ins = act.activation(dst, bank[b][0:rows, n, :, :], ACT.Copy)
                ins.then_inc(evac_ok, 1)

            gu = wgu[:, :, :, :, :].rearrange("p l k c n -> p l k (c n)")
            for unit in range(2):
                evac(unit, unit, [(wgu[:, :, kc, unit, :], P) for kc in range(KC)])
            norm.act_hi(act, 0)
            win_hi()
            with act.Fori(1, GUC // 2) as i:
                for b in range(2):
                    cols = bass.ds(i * (2 * P) + b * P, P)
                    evac(b, i * 2 + b, [(gu[:, :, kc, cols], P) for kc in range(KC)])
            evac(0, GUC - 1, [(wgu[:, :, kc, GUC - 1, :], P) for kc in range(KC)])
            act.wait_ge(zeroed, 2)
            for n, (m, _, _, fs) in enumerate(DOWN):
                evac((GUC + n) % 2, GUC + n, [(wd[0:rows, :, f, P * m:P * m + P], rows) for f, rows in fs])
            act.wait_ge(wout_in, 16)
            act.wait_ge(small_in, 16 * (7 + HG))
            for k in range(4):
                act.activation(wout_raw[:, k, :], wout_raw[:, k, :], ACT.Copy,
                               scale=T["norm_w"][:, k:k + 1]).then_inc(wout_s, 1)
            act.wait_ge(wout_s, 4)
            act.activation(wout[:, 0, :, :], wout_raw[:, :, :], ACT.Copy).then_inc(split_hi, 1)

        @block.tensor
        def _(pe):
            pe.wait_ge(diag_ok, 2 * LUT)

            def lookup(b, unit):
                pe.wait_ge(evac_ok, unit + 1)
                for n in range(2):
                    for k in range(LUT):
                        if n == 0 and k % 4 == 0:
                            pe.wait_ge(mask_ok, unit * LUT + k + 4)
                        ins = pe.matmul(bank[b][:, n, :, :], mask[b][:, k, P * n:P * n + P], diag[:, k, :, :],
                                        start=k == 0, stop=k == LUT - 1)
                ins.then_inc(prod_ok, 1)

            for unit in range(2):
                lookup(unit, unit)
            norm.pe_transpose(pe, 0)
            with pe.Fori(1, GUC // 2) as i:
                for b in range(2):
                    lookup(b, i * 2 + b)
            for unit in range(GUC - 1, GUC + len(DOWN)):
                lookup(unit % 2, unit)


class Norm:

    def __init__(self, nc, ctx, T, tag, side="left"):
        sb = lambda n, s, d=F32: ctx.enter_context(nc.sbuf_tensor(tag + n, s, d, side=side))
        sem = lambda n: ctx.enter_context(nc.semaphore(tag + n))
        self.T = T
        self.stats = sb("stats", [P, GT, 6])
        self.mv = sb("mv", [P, GT, 2])
        self.ve = sb("ve", [P, GT])
        self.rstd = sb("rstd", [P, GT])
        self.xn = sb("xn", [P, GT, HID])
        self.xT = sb("xT", [P, 2, KC, L], F32R)
        self.base = 0
        self.pt = [ctx.enter_context(nc.psum_tensor(f"{tag}pt{k}", [P, GN], F32)) for k in range(KC)]
        self.stat_ok, self.mv_ok, self.ve_ok, self.rstd_ok = map(sem, ("stat_ok", "mv_ok", "ve_ok", "rstd_ok"))
        self.xn_ok, self.pt_ok, self.hi_ok, self.lo_ok = map(sem, ("xn_ok", "pt_ok", "hi_ok", "lo_ok"))
        self.stat_seen = sem("stat_seen")

    def rows(self, g, t):
        g = g % GROUPS if isinstance(g, int) else g
        x = self.T["x_res"][:, :, :].rearrange("p t c -> p (t c)")
        return x[:, bass.ds(g * (GT * HID) + t * HID, HID)]

    def tokens(self, g):
        return bass.ds((g % GROUPS if isinstance(g, int) else g) * GN, GN)

    def dve_start(self, dve):
        dve.sem_inc(self.lo_ok, KC)
        dve.sem_inc(self.pt_ok, 1)

    def dve_stats(self, dve, g):
        for t in range(GT):
            dve.bn_stats(self.stats[:, t, :], self.rows(g, t)).then_inc(self.stat_ok, 1)
        dve.wait_ge(self.stat_ok, (g + self.base) * GT + GT)
        dve.sem_inc(self.stat_seen, 1)
        for t in range(GT):
            dve.bn_aggr(self.mv[:, t, :], self.stats[:, t, :]).then_inc(self.mv_ok, 1)
        dve.wait_ge(self.mv_ok, (g + self.base) * GT + GT)
        dve.tensor_scalar(self.ve[:, :], self.mv[:, :, 1], EPS, None, ALU.add).then_inc(self.ve_ok, 1)

    def pool_rstd(self, pool, g):
        pool.wait_ge(self.ve_ok, g + self.base + 1)
        pool.tensor_tensor(self.rstd[:, :], self.ve[:, :], self.T["m_half"][:, 0:GT], ALU.pow).then_inc(self.rstd_ok, 1)

    def dve_xn(self, dve, g):
        dve.wait_ge(self.rstd_ok, g + self.base + 1)
        dve.wait_ge(self.pt_ok, g + self.base + 1)
        for t in range(GT):
            dve.tensor_scalar(self.xn[:, t, :], self.rows(g, t), self.mv[:, t, 0:1], self.rstd[:, t:t + 1],
                              ALU.subtract, ALU.mult).then_inc(self.xn_ok, 1)

    def pe_transpose(self, pe, g):
        pe.wait_ge(self.xn_ok, (g + self.base) * GT + GT)
        pe.wait_ge(self.lo_ok, (g + self.base) * KC + KC)
        for kc in range(KC):
            for t in range(GT):
                last = pe.transpose(self.pt[kc][:, P * t:P * t + P], self.xn[:, t, P * kc:P * kc + P],
                                    self.T["ident"][:, :])
        last.then_inc(self.pt_ok, 1)

    def act_hi(self, act, g):
        act.wait_ge(self.pt_ok, g + self.base + 2)
        for kc in range(KC):
            act.activation(self.xT[:, 0, kc, self.tokens(g)], self.pt[kc][:, :], ACT.Copy).then_inc(self.hi_ok, 1)

    def dve_lo(self, dve, g):
        for kc in range(KC):
            dve.wait_ge(self.hi_ok, (g + self.base) * KC + kc + 1)
            dve.tensor_tensor(self.xT[:, 1, kc, self.tokens(g)], self.pt[kc][:, :], self.xT[:, 0, kc, self.tokens(g)].bitcast(F32),
                              ALU.subtract).then_inc(self.lo_ok, 1)

    def pe_ready(self, pe, g, kc):
        pe.wait_ge(self.lo_ok, (g + self.base) * KC + kc + 1 + KC)


def over_groups(eng, body, last_too=False):
    with eng.Fori(0, GROUPS - 1) as g:
        body(g, True)
    body(GROUPS - 1, last_too)


def build_ffn(nc, T, tag, norm, out=None):
    with ExitStack() as ctx:
        sb = lambda n, s, d=F32: ctx.enter_context(nc.sbuf_tensor(tag + n, s, d))
        ps = lambda n, s: ctx.enter_context(nc.psum_tensor(tag + n, s, F32))
        sem = lambda n: ctx.enter_context(nc.semaphore(tag + n))
        first = out is None
        hT = sb("hT", [P, 2, FCH, GN], F32R)
        sg = [sb(f"sg{b}", [P, GN]) for b in range(2)]
        h = sb("h", [P, GN])
        gate = [ps(f"gate{b}", [P, GN]) for b in range(2)]
        up = [ps(f"up{b}", [P, GN]) for b in range(2)]
        down = [ps(f"down{b}", [P, 2, HID]) for b in range(2)]
        gate_ok, up_ok, silu_ok, h_ok, h_hi, h_lo = map(sem, ("gate_ok", "up_ok", "silu_ok", "h_ok", "h_hi", "h_lo"))
        down_ok, res_ok, hz, stored = map(sem, ("down_ok", "res_ok", "hz", "stored"))
        wgu, wd, x_res = T["wgu"], T["wd"], T["x_res"]
        xflat = x_res[:, :, :].rearrange("p t c -> p (t c)")
        PAIRS = GT // 2
        block = ctx.enter_context(nc.Block())

        def rows(c):
            return P if c < FCH - 1 else FLAST

        @block.vector
        def _(dve):
            dve.sem_inc(h_ok, 2)
            if not first:
                norm.dve_start(dve)
                norm.dve_stats(dve, 0)
                norm.dve_xn(dve, 0)
                norm.dve_lo(dve, 0)

            def body(g, ahead):
                for c in range(FCH):
                    r = rows(c)
                    dve.wait_ge(silu_ok, g * FCH + c + 1)
                    if c < FCH - 1:
                        dve.wait_ge(up_ok, g * (FCH - 1) + c + 1)
                        other = up[c % 2][:, :]
                    else:
                        other = gate[c % 2][64:64 + r, :]
                    dve.tensor_tensor(h[0:r, :], sg[c % 2][0:r, :], other, ALU.mult).then_inc(h_ok, 1)
                    dve.wait_ge(h_hi, g * FCH + c + 1)
                    dve.tensor_tensor(hT[0:r, 1, c, :], h[0:r, :], hT[0:r, 0, c, :].bitcast(F32),
                                      ALU.subtract).then_inc(h_lo, 1)
                    if ahead and c == 0:
                        norm.dve_stats(dve, g + 1)
                    if ahead and c == 2:
                        norm.dve_xn(dve, g + 1)
                    dve.wait_ge(h_lo, g * FCH + c + 1)
                if ahead:
                    norm.dve_lo(dve, g + 1)
                for j in range(PAIRS):
                    dve.wait_ge(down_ok, g * PAIRS + j + 1)
                    xt = xflat[:, bass.ds(g * (GT * HID) + j * (2 * HID), 2 * HID)]
                    dve.scalar_tensor_tensor(xt, down[j][:, :, :].rearrange("p t c -> p (t c)"), 0.5, xt,
                                             ALU.mult, ALU.add).then_inc(res_ok, 1)

            over_groups(dve, body, first)

        @block.gpsimd
        def _(pool):
            pool.memset(hT[:, 0, FCH - 1, :].bitcast(F32), 0.0).then_inc(hz, 1)
            pool.memset(hT[:, 1, FCH - 1, :].bitcast(F32), 0.0).then_inc(hz, 1)
            if not first:
                norm.pool_rstd(pool, 0)
            with pool.Fori(0, GROUPS - 1) as g:
                norm.pool_rstd(pool, g + 1)
            if first:
                norm.pool_rstd(pool, GROUPS)

        @block.scalar
        def _(act):
            act.wait_ge(hz, 2)
            if not first:
                norm.act_hi(act, 0)

            def body(g, ahead):
                for c in range(FCH):
                    r = rows(c)
                    act.wait_ge(gate_ok, g * FCH + c + 1)
                    act.activation(sg[c % 2][0:r, :], gate[c % 2][0:r, :], ACT.Silu).then_inc(silu_ok, 1)
                    act.wait_ge(h_ok, g * FCH + c + 3)
                    act.activation(hT[0:r, 0, c, :], h[0:r, :], ACT.Copy).then_inc(h_hi, 1)
                if ahead:
                    norm.act_hi(act, g + 1)

            over_groups(act, body, first)

        @block.tensor
        def _(pe):
            pe.sem_inc(res_ok, PAIRS)
            pe.wait_ge(hz, 2)
            if not first:
                norm.pe_transpose(pe, 0)
            x_hi, x_lo = norm.xT[:, 0], norm.xT[:, 1]

            def body(g, ahead):
                for c in range(FCH):
                    pe.wait_ge(h_ok, g * FCH + c + 1)
                    parts = [(gate[c % 2], c, gate_ok), (up[c % 2], 5 + c, up_ok)] if c < FCH - 1 \
                        else [(gate[c % 2], GUC - 1, gate_ok)]
                    for bank, wc, done in parts:
                        for kc in range(KC):
                            if wc == 0:
                                norm.pe_ready(pe, g, kc)
                            last = split_mm(pe, bank[:, :], wgu[:, 0, kc, wc, :], wgu[:, 1, kc, wc, :],
                                            x_hi[:, kc, norm.tokens(g)], x_lo[:, kc, norm.tokens(g)],
                                            kc == 0, kc == KC - 1)
                        last.then_inc(done, 1)
                if ahead:
                    norm.pe_transpose(pe, g + 1)
                LASTC = (FCH - 1,)
                parts = ((0, 0, range(FCH - 1)), (1, 0, range(FCH - 1)), (0, 0, LASTC), (0, 1, range(FCH)),
                         (1, 0, LASTC), (1, 1, range(FCH)))
                for n, (j, t, chunks) in enumerate(parts):
                    if n < PAIRS:
                        pe.wait_ge(res_ok, g * PAIRS + j + 1)
                    tok = slice(P * (2 * j + t), P * (2 * j + t) + P)
                    for c in chunks:
                        if n == 0 or n == 2:
                            pe.wait_ge(h_lo, g * FCH + c + 1)
                        last = split_mm(pe, down[j][:, t, :], hT[:, 0, c, tok], hT[:, 1, c, tok],
                                        wd[:, 0, c, :], wd[:, 1, c, :], c == 0, c == FCH - 1)
                    if t:
                        last.then_inc(down_ok, 1)

            over_groups(pe, body, first)

        @block.sync
        def _(sp):
            if out is None:
                for name in ("wgu", "wd"):
                    chip = T[name][tuple([slice(None)] * len(T[name].shape))].bitcast(F32)
                    sp.dma_start(T[name + "_dram"], chip).then_inc(stored, 16)
                sp.wait_ge(stored, 32)
            else:
                dst = out[0].rearrange("(t p) c -> p t c", p=P)
                for g in range(GROUPS):
                    sp.wait_ge(res_ok, (g + 2) * PAIRS)
                    sp.dma_start(dst[:, g * GT:g * GT + GT, :], x_res[:, g * GT:g * GT + GT, :]).then_inc(stored, 16)
                sp.wait_ge(stored, 16 * GROUPS)


def build_in_proj(nc, T, norm):
    with ExitStack() as ctx:
        sb = lambda n, s, d=F32: ctx.enter_context(nc.sbuf_tensor(n, s, d))
        sem = lambda n: ctx.enter_context(nc.semaphore(n))
        norm.base = GROUPS
        HALO = KCONV - 1
        pre = sb("pre", [P, XCH, HALO + GN])
        prod = sb("prod", [P, GN])
        bank = [ctx.enter_context(nc.psum_tensor(f"pj{b}", [P, GN], F32)) for b in range(4)]
        mm_ok, ev_ok, carry_v, carry_p, tap_v, tap_p = map(sem, ("mm_ok", "ev_ok", "carry_v", "carry_p", "tap_v", "tap_p"))
        w_ok, prod_ok, seen = map(sem, ("w_ok", "prod_ok", "seen"))
        win, cv, zs = T["win"], T["cv"], T["zs"]
        cw, cb = T["conv_w"], T["conv_b"]
        ORDER = (10, 8, 9, 4, 5, 6, 7, 0, 1, 2, 3)
        V_CH, P_CH = (0, 1, 2, 3), (4, 5)
        EV_FREE = 3
        block = ctx.enter_context(nc.Block())

        def evacuated(g, place):
            return g * PCH + (place + 1 + EV_FREE)

        @block.vector
        def _(dve):
            dve.tensor_scalar(cw[:, :, :], cw[:, :, :], MUP_X, None, ALU.mult).then_inc(w_ok, 1)
            dve.memset(pre[:, 0:len(V_CH), 0:HALO], 0.0).then_inc(carry_v, len(V_CH))
            dve.wait_ge(w_ok, 1)

            def body(g, ahead):
                if ahead:
                    norm.dve_stats(dve, g + 1)
                    norm.dve_xn(dve, g + 1)
                n = 0
                for c in V_CH:
                    dve.wait_ge(ev_ok, evacuated(g, ORDER.index(4 + c)))
                    dst = cv[:, c, bass.ds(g * GN, GN)]
                    for k in range(HALO):
                        if k:
                            dve.wait_ge(tap_v, g * (HALO * len(V_CH)) + n)
                        dve.scalar_tensor_tensor(dst, pre[:, c, k:k + GN], cw[:, c, k:k + 1], dst,
                                                 ALU.mult, ALU.add).then_inc(tap_v, 1)
                        n += 1
                    dve.wait_ge(tap_v, g * (HALO * len(V_CH)) + n)
                    dve.tensor_copy(pre[:, c, 0:HALO], pre[:, c, GN:GN + HALO]).then_inc(carry_v, 1)
                if ahead:
                    norm.dve_lo(dve, g + 1)

            over_groups(dve, body)

        @block.gpsimd
        def _(pool):
            pool.memset(pre[:, len(V_CH):XCH, 0:HALO], 0.0).then_inc(carry_p, len(P_CH))
            pool.wait_ge(w_ok, 1)

            def after(sem, value):
                pool.wait_ge(sem, value)
                pool.sem_inc(seen, 1)

            def body(g, ahead):
                if ahead:
                    norm.pool_rstd(pool, g + 1)
                n = 0
                for j, c in enumerate(P_CH):
                    dst = cv[:, c, bass.ds(g * GN, GN)]
                    after(ev_ok, evacuated(g, ORDER.index(4 + c)))
                    for k in range(HALO):
                        if n or j:
                            after(tap_p, g * (HALO * len(P_CH)) + n)
                        pool.tensor_scalar(prod[:, :], pre[:, c, k:k + GN], cw[:, c, k:k + 1], None,
                                           ALU.mult).then_inc(prod_ok, 1)
                        n += 1
                        after(prod_ok, g * (HALO * len(P_CH)) + n)
                        pool.tensor_tensor(dst, dst, prod[:, :], ALU.add).then_inc(tap_p, 1)
                    after(tap_p, g * (HALO * len(P_CH)) + n)
                    pool.tensor_copy(pre[:, c, 0:HALO], pre[:, c, GN:GN + HALO]).then_inc(carry_p, 1)

            over_groups(pool, body)

        @block.scalar
        def _(act):
            act.sem_inc(ev_ok, EV_FREE)
            act.wait_ge(w_ok, 1)

            def body(g, ahead):
                for place, c in enumerate(ORDER):
                    act.wait_ge(mm_ok, g * PCH + place + 1)
                    src = bank[place % 4][:, :]
                    if c < 4:
                        act.activation(zs[:, c, bass.ds(g * GN, GN)], src, ACT.Silu, scale=MUP_Z).then_inc(ev_ok, 1)
                    elif c < 4 + XCH:
                        x = c - 4
                        if x in V_CH:
                            act.wait_ge(carry_v, g * len(V_CH) + V_CH.index(x) + 1)
                        else:
                            act.wait_ge(carry_p, g * len(P_CH) + P_CH.index(x) + 1)
                        act.activation(pre[:, x, HALO:HALO + GN], src, ACT.Copy)
                        act.activation(cv[:, x, bass.ds(g * GN, GN)], src, ACT.Identity, scale=cw[:, x, HALO:HALO + 1],
                                       bias=cb[:, x:x + 1]).then_inc(ev_ok, 1)
                    else:
                        act.activation(T["dt_raw"][:, bass.ds(g * GN, GN)], src, ACT.Identity,
                                       bias=T["dt_b"][:, 0:1]).then_inc(ev_ok, 1)
                    if ahead and place == 8:
                        norm.act_hi(act, g + 1)

            over_groups(act, body)

        @block.tensor
        def _(pe):
            x_hi, x_lo = norm.xT[:, 0], norm.xT[:, 1]

            def body(g, ahead):
                for place, c in enumerate(ORDER):
                    last_user = place - 4 if place >= 4 else PCH - 4 + (place + 1) % 4 - PCH
                    pe.wait_ge(ev_ok, g * PCH + max(last_user + 1 + EV_FREE, 1))
                    for kc in range(KC):
                        if place == 0:
                            norm.pe_ready(pe, g, kc)
                        last = split_mm(pe, bank[place % 4][:, :], win[:, 0, kc, c, :], win[:, 1, kc, c, :],
                                        x_hi[:, kc, norm.tokens(g)], x_lo[:, kc, norm.tokens(g)], kc == 0, kc == KC - 1)
                    last.then_inc(mm_ok, 1)
                    if ahead and place == 6:
                        norm.pe_transpose(pe, g + 1)

            over_groups(pe, body)


def build_decay(nc, T):
    with ExitStack() as ctx:
        sb = lambda n, s, d=F32: ctx.enter_context(nc.sbuf_tensor(n, s, d))
        sem = lambda n: ctx.enter_context(nc.semaphore(n))
        H = L // 2
        HB = BLOCKS // 2
        HT = TILES // 2
        e, u, ln, dt, a, a0, cp = (sb(n, [P, H]) for n in ("e_abs", "one_e", "ln_u", "dtT", "aT", "a0T", "cpT"))
        A = sb("A_neg", [P, 1])
        eA = sb("eA", [P, 1])
        dend = sb("dend", [P, HB])
        dendT = sb("dendT", [HB, P])
        pt_dt = ctx.enter_context(nc.psum_tensor("pt_dt", [P, HT, 2, HEADS], F32))
        pt_cp = ctx.enter_context(nc.psum_tensor("pt_cp", [P, HT, 2, HEADS], F32))
        pt_d = ctx.enter_context(nc.psum_tensor("pt_d", [HB, P], F32))
        abs_ok, exp_ok, ln_ok, eA_ok, a_ok, u_ok, nd_ok, s_ok, dt_ok, A_ok = map(sem, (
            "abs_ok", "exp_ok", "ln_ok", "eA_ok", "a_ok", "u_ok", "nd_ok", "s_ok", "dt_ok", "A_ok"))
        a0_ok, az_ok, cp_ok, dend_ok, dendT_ok, zero_ok, dma_ok = map(sem, (
            "a0_ok", "az_ok", "cp_ok", "dend_ok", "dendT_ok", "zero_ok", "dma_ok"))
        tr_d, tr_dt, tr_cp = map(sem, ("tr_d", "tr_dt", "tr_cp"))
        halves = [(k, slice(HEADS * k, HEADS * k + HEADS)) for k in range(2)]
        raw = T["dt_raw"]
        block = ctx.enter_context(nc.Block())

        def store_a(eng, k, r):
            eng.wait_ge(az_ok, 1)
            eng.dma_start(T["a_dram"].rearrange("b h i -> h b i")[:, HB * k:HB * k + HB, :],
                          a[r, :].rearrange("h (b i) -> h b i", i=Q)).then_inc(dma_ok, 16)

        @block.vector
        def _(dve):
            dve.wait_ge(exp_ok, 1)
            dve.tensor_scalar(u[:, :], e[:, :], 1.0, None, ALU.add).then_inc(u_ok, 1)
            dve.wait_ge(u_ok, 1)
            dve.scalar_tensor_tensor(e[:, :], u[:, :], 1.0, e[:, :], ALU.subtract, ALU.subtract).then_inc(nd_ok, 1)
            dve.wait_ge(eA_ok, 1)
            dve.tensor_scalar(A[:, :], eA[:, :], -1.0, None, ALU.mult).then_inc(A_ok, 1)
            dve.wait_ge(nd_ok, 1)
            dve.wait_ge(ln_ok, 1)
            dve.tensor_tensor(ln[:, :], ln[:, :], e[:, :], ALU.subtract).then_inc(s_ok, 1)
            dve.wait_ge(s_ok, 1)
            for k, r in halves:
                dve.scalar_tensor_tensor(dt[r, :], raw[r, H * k:H * k + H], 0.0, ln[r, :], ALU.max, ALU.add
                                         ).then_inc(dt_ok, 1)
            dve.wait_ge(a_ok, 1)
            dve.wait_ge(zero_ok, 1)
            dve.tensor_copy(a0[:, 0:H:Q], a[:, 0:H:Q]).then_inc(a0_ok, 1)
            dve.wait_ge(a0_ok, 1)
            dve.memset(a[:, 0:H:Q], 0.0).then_inc(az_ok, 1)
            dve.wait_ge(az_ok, 1)
            dve.tensor_tensor_scan(cp[:, :], a[:, :], a0[:, :], 0.0, ALU.mult, ALU.add).then_inc(cp_ok, 1)
            dve.wait_ge(cp_ok, 1)
            dve.tensor_copy(dend[:, :], cp[:, Q - 1:H:Q]).then_inc(dend_ok, 1)
            dve.wait_ge(tr_d, 1)
            dve.tensor_copy(dendT[:, :], pt_d[:, :]).then_inc(dendT_ok, 1)
            dve.wait_ge(tr_cp, 1)
            for b in range(NB // 2):
                for q in range(4):
                    dve.tensor_copy(
                        T["cp_g"][Q * q:Q * q + Q, :, b, :].rearrange("p (k t) h -> p k t h", k=2),
                        pt_cp[Q * b:Q * b + Q, :, :, HG * q:HG * q + HG].rearrange("p t k h -> p k t h"))

        @block.scalar
        def _(act):
            for k, r in halves:
                act.activation(e[r, :], raw[r, H * k:H * k + H], ACT.Abs).then_inc(abs_ok, 1)
            act.wait_ge(abs_ok, 2)
            act.activation(e[:, :], e[:, :], ACT.Exp, scale=-1.0).then_inc(exp_ok, 1)
            act.activation(eA[:, :], T["a_log"][:, :], ACT.Exp).then_inc(eA_ok, 1)
            act.wait_ge(u_ok, 1)
            act.activation(ln[:, :], u[:, :], ACT.Ln).then_inc(ln_ok, 1)
            act.wait_ge(A_ok, 1)
            act.wait_ge(dt_ok, 2)
            act.activation(a[:, :], dt[:, :], ACT.Exp, scale=A[:, 0:1]).then_inc(a_ok, 1)
            store_a(act, *halves[1])
            act.wait_ge(tr_dt, 1)
            act.activation(T["dt_tok"][:, :, :].rearrange("p (k t) h -> p k t h", k=2),
                           pt_dt[:, :, :, :].rearrange("p t k h -> p k t h"), ACT.Copy)
            act.wait_ge(tr_cp, 1)
            for b in range(NB // 2, NB):
                for q in range(4):
                    act.activation(
                        T["cp_g"][Q * q:Q * q + Q, :, b, :].rearrange("p (k t) h -> p k t h", k=2),
                        pt_cp[Q * b:Q * b + Q, :, :, HG * q:HG * q + HG].rearrange("p t k h -> p k t h"), ACT.Copy)

        @block.gpsimd
        def _(pool):
            pool.memset(a0[:, :], 0.0).then_inc(zero_ok, 1)

        @block.tensor
        def _(pe):
            pe.wait_ge(dt_ok, 2)
            for t in range(HT):
                last = pe.transpose(pt_dt[:, t, :, :].rearrange("p k h -> p (k h)"), dt[:, P * t:P * t + P],
                                    T["ident"][:, :])
            last.then_inc(tr_dt, 1)
            pe.wait_ge(cp_ok, 1)
            for t in range(HT):
                last = pe.transpose(pt_cp[:, t, :, :].rearrange("p k h -> p (k h)"), cp[:, P * t:P * t + P],
                                    T["ident"][:, :])
            last.then_inc(tr_cp, 1)
            pe.wait_ge(dend_ok, 1)
            pe.transpose(pt_d[:, :], dend[:, :], T["ident"][:, :]).then_inc(tr_d, 1)

        @block.sync
        def _(sp):
            store_a(sp, *halves[0])
            sp.wait_ge(dendT_ok, 1)
            sp.dma_start(T["dend_dram"].rearrange("(k b) h -> b k h", k=2),
                         dendT[:, :].rearrange("b (k h) -> b k h", k=2)).then_inc(dma_ok, 16)
            sp.wait_ge(dma_ok, 48)


def build_scan(nc, T):
    with ExitStack() as ctx:
        sb = lambda n, s, d=F32: ctx.enter_context(nc.sbuf_tensor(n, s, d))
        ps = lambda n, s: ctx.enter_context(nc.psum_tensor(n, s, F32))
        sem = lambda n: ctx.enter_context(nc.semaphore(n))
        HI = HEADS * Q
        d0 = [sb(f"d0_{b}", [P, HI]) for b in range(2)]
        dend = [sb(f"dend_{b}", [P, NB, HEADS]) for b in range(2)]
        eye_q = sb("eye_q", [P, HG * Q])
        lmat = sb("lmat", [P, HEADS, Q])
        mmat = sb("mmat", [P, HEADS, Q])
        xbd = sb("xbd", [P, HEADS, NB, PD])
        xT = [sb(f"xs_{b}", [P, 4, P]) for b in range(4)]
        bc = [sb(f"bc_{b}", [P, 2, P]) for b in range(4)]
        xdt, xr, tmp, y, yf, sq, u = (sb(n, [P, INTER]) for n in ("xdt", "xr", "tmp", "y", "yf", "sq", "u"))
        bm = [sb(f"bm_{b}", [P, NB, NS]) for b in range(2)]
        gs = [sb(f"gs_{b}", [P, Q]) for b in range(2)]
        s0 = [sb(f"s0_{b}", [P, INTER]) for b in range(2)]
        s123 = sb("s123", [P, NB - 1, INTER])
        ssum = sb("ssum", [P, P])
        ve = sb("ve_y", [P, 1])
        rstd = sb("rstd_y", [P, 1])
        uh = sb("uh", [P, 2, 4, P], F32R)
        X, BG = ps("X", [P, INTER]), ps("BG", [P, NS + Q + 1])
        new = [ps(f"new{b}", [P, INTER]) for b in range(2)]
        intra, yint = ps("intra", [P, NB, HG, PD]), ps("yint", [P, NB, HG * PD])
        ytr, outp = ps("ytr", [P, NB, P]), ps("outp", [P, HID])
        names = ("scan_ok", "smul_ok", "xs_ok", "bc_ok", "tr_ok", "gs_ok", "bm_ok", "xdt_ok", "xbd_ok", "xr_ok",
                 "m_ok", "new_ok", "add_ok", "yint_ok", "intra_ok", "yi_ok", "y_ok", "ytr_ok", "yf_ok", "sq_ok",
                 "u_ok", "uhi_ok", "ulo_ok", "red_ok", "ss_ok", "ve_ok", "rs_ok", "out_ok", "res_ok", "set_ok",
                 "eye_ok")
        s = {n: sem("c_" + n) for n in names}
        d0_in = [sem(f"d0_in{b}") for b in range(2)]
        dend_in = [sem(f"dend_in{b}") for b in range(2)]
        loaded = sem("ffn_loaded")
        FREE = dict(scan_ok=2, smul_ok=8, m_ok=2, yint_ok=2, new_ok=4, intra_ok=1, xdt_ok=1, bm_ok=4, gs_ok=1,
                    add_ok=2, y_ok=1, yf_ok=16, res_ok=1, xbd_ok=4, ytr_ok=1, sq_ok=1, uhi_ok=1, ss_ok=1,
                    out_ok=1, u_ok=1, ulo_ok=1, red_ok=1, ve_ok=2)
        PER = dict(smul_ok=4, new_ok=4, bm_ok=4, add_ok=4, xbd_ok=4, yf_ok=4)
        cv, zs, x_res, wout = T["cv"], T["zs"], T["x_res"], T["wout"]
        block = ctx.enter_context(nc.Block())

        def times(tile, mul):
            i, c = tile
            return c * mul if i is None else i * (4 * mul) + c * mul

        def count(name, tile, after=0, part=0):
            i, c = tile
            per = PER.get(name, 1)
            base = FREE.get(name, 0) + (part if part else per)
            return times((i, c + after), per) + base

        def wait(eng, name, tile, after=0, part=0):
            value = count(name, tile, after, part)
            if tile[0] is not None or value > 0:
                eng.wait_ge(s[name], value)

        def half(tile):
            i, c = tile
            return c // 2 + 1 if i is None else i * 2 + c // 2 + 1

        def pipeline(eng, step):
            for t in range(2):
                step(t, None, True, t >= 1, False)
            with eng.Fori(0, (TILES - 4) // 4) as i:
                for k in range(4):
                    step(2 + k, i, True, True, True)
            for t in range(TILES - 2, TILES + 2):
                step(t, None, t < TILES, t - 1 < TILES, True)

        @block.sync
        def _(sp):
            with sp.Fori(0, TILES // 4) as i:
                for c in range(4):
                    tile = (i, c)
                    wait(sp, "scan_ok", tile, -2)
                    for b in range(NB):
                        src = T["a_dram"].rearrange("b h i -> b (h i)")[bass.ds(i * 16 + c * 4 + b, 1), :]
                        sp.dma_start(d0[c % 2][Q * b:Q * b + Q, :], src.broadcast_to([Q, HI])).then_inc(d0_in[c % 2], 16)
                    wait(sp, "smul_ok", tile, -2)
                    src = T["dend_dram"].rearrange("(t b) h -> t (b h)", b=NB)[bass.ds(i * 4 + c, 1), :]
                    sp.dma_start(dend[c % 2][:, :, :].rearrange("p b h -> p (b h)"),
                                 src.broadcast_to([P, NB * HEADS])).then_inc(dend_in[c % 2], 16)
            wait(sp, "xs_ok", (None, TILES - 1))
            wait(sp, "bc_ok", (None, TILES - 1))
            for name in ("wgu", "wd"):
                chip = T[name][tuple([slice(None)] * len(T[name].shape))].bitcast(F32)
                sp.dma_start(chip, T[name + "_dram"]).then_inc(loaded, 16)
            sp.wait_ge(loaded, 32)

        @block.scalar
        def _(act):
            act.sem_inc(s["bm_ok"], FREE["bm_ok"])
            act.sem_inc(s["gs_ok"], FREE["gs_ok"])
            act.sem_inc(s["xbd_ok"], FREE["xbd_ok"])
            act.sem_inc(s["sq_ok"], FREE["sq_ok"])
            act.sem_inc(s["uhi_ok"], FREE["uhi_ok"])
            act.wait_ge(s["set_ok"], 3)

            def silus(n):
                tok = bass.ds(times(n, P), P)
                wait(act, "yf_ok", n, -4)
                act.activation(xT[n[1] % 4][:, :, :], cv[:, 0:4, tok], ACT.Silu).then_inc(s["xs_ok"], 1)
                wait(act, "yint_ok", n, -4)
                act.activation(bc[n[1] % 4][:, :, :], cv[:, 4:6, tok], ACT.Silu).then_inc(s["bc_ok"], 1)

            def step(c, i, do_a, do_b, do_c):
                a, z = (i, c), (i, c - 2)
                if do_a:
                    wait(act, "tr_ok", a)
                    wait(act, "m_ok", a, -2)
                    act.activation(gs[c % 2][:, :], BG[:, NS:NS + Q], ACT.Copy).then_inc(s["gs_ok"], 1)
                    wait(act, "new_ok", a, -2)
                    for b in range(NB):
                        r = slice(Q * b, Q * b + Q)
                        act.activation(bm[c % 2][r, b, :], BG[r, 0:NS], ACT.Copy).then_inc(s["bm_ok"], 1)
                if do_c:
                    wait(act, "yf_ok", z)
                    wait(act, "red_ok", z, -1)
                    act.activation(sq[:, :], yf[:, :], ACT.Square).then_inc(s["sq_ok"], 1)
                    wait(act, "u_ok", z)
                    wait(act, "out_ok", z, -1)
                    act.activation(uh[:, 0, :, :], u[:, :].rearrange("p (g t) -> p g t", g=4), ACT.Copy
                                   ).then_inc(s["uhi_ok"], 1)
                if do_a:
                    if i is not None or c < TILES - 1:
                        silus((i, c + 1))
                    wait(act, "xdt_ok", a)
                    wait(act, "intra_ok", a, -1)
                    for b in range(NB):
                        r = slice(Q * b, Q * b + Q)
                        act.activation(xbd[r, :, b, :], xdt[r, :].rearrange("p (h d) -> p h d", d=PD), ACT.Copy
                                       ).then_inc(s["xbd_ok"], 1)

            silus((None, 0))
            pipeline(act, step)

        @block.vector
        def _(dve):
            for n in ("scan_ok", "xdt_ok", "y_ok", "yf_ok", "res_ok", "u_ok", "ulo_ok", "red_ok", "ve_ok"):
                dve.sem_inc(s[n], FREE[n])
            dve.memset(s0[0][:, :], 0.0).then_inc(s["add_ok"], FREE["add_ok"])
            dve.wait_ge(s["eye_ok"], 2)

            def add(b_, c, b):
                wait(dve, "new_ok", b_, 0, b + 1)
                wait(dve, "smul_ok", b_, 0, b + 1)
                dst = s123[:, b, :] if b < NB - 1 else s0[c % 2][:, :]
                dve.tensor_tensor(dst, tmp[:, :], new[b % 2][:, :], ALU.add).then_inc(s["add_ok"], 1)

            def decay_scan(c, pieces):
                lflat = lmat[:, :, :].rearrange("p h i -> p (h i)")
                for q in pieces:
                    cols = slice(HG * Q * q, HG * Q * (q + 1))
                    ins = dve.tensor_tensor_scan(lflat[:, cols], d0[c % 2][:, cols], eye_q[:, :], 0.0,
                                                 ALU.mult, ALU.add)
                return ins

            def step(c, i, do_a, do_b, do_c):
                a, b_, z = (i, c), (i, c - 1), (i, c - 2)
                if do_a:
                    wait(dve, "tr_ok", a)
                    wait(dve, "xbd_ok", a, -1)
                    wait(dve, "xr_ok", a, -1)
                    dt = T["dt_tok"][:, :, :].rearrange("p t h -> p (t h)")[:, bass.ds(times(a, HEADS), HEADS)]
                    dve.tensor_tensor(xdt[:, :].rearrange("p (h d) -> p h d", d=PD),
                                      X[:, :].rearrange("p (h d) -> p h d", d=PD),
                                      dt.unsqueeze(2).broadcast_to([P, HEADS, PD]), ALU.mult).then_inc(s["xdt_ok"], 1)
                if do_c:
                    wait(dve, "ytr_ok", z)
                    wait(dve, "sq_ok", z, -1)
                    wait(dve, "u_ok", z, -1)
                    for g in range(4):
                        dve.scalar_tensor_tensor(
                            yf[:, P * g:P * g + P].rearrange("p (b t) -> p b t", b=NB),
                            xT[(c - 2) % 4][:, g, :].rearrange("p (b t) -> p b t", b=NB), T["d_ch"][:, g:g + 1],
                            ytr[:, :, Q * g:Q * g + Q], ALU.mult, ALU.add).then_inc(s["yf_ok"], 1)
                    wait(dve, "yf_ok", z)
                    wait(dve, "uhi_ok", z, -1)
                    wait(dve, "ulo_ok", z, -1)
                    dve.tensor_tensor(u[:, :].rearrange("p (g t) -> p g t", g=4),
                                      yf[:, :].rearrange("p (g t) -> p g t", g=4),
                                      zs[:, :, bass.ds(times(z, P), P)], ALU.mult).then_inc(s["u_ok"], 1)
                if do_b:
                    wait(dve, "yint_ok", b_, -1)
                    add(b_, c, 0)
                if do_c:
                    wait(dve, "sq_ok", z)
                    wait(dve, "ss_ok", z, -1)
                    dve.tensor_reduce(ssum[:, :], sq[:, :].rearrange("p (g t) -> p t g", g=4),
                                      mybir.AxisListType.X, ALU.add).then_inc(s["red_ok"], 1)
                    wait(dve, "uhi_ok", z)
                    dve.tensor_tensor(uh[:, 1, :, :].rearrange("p g t -> p (g t)"), u[:, :],
                                      uh[:, 0, :, :].bitcast(F32).rearrange("p g t -> p (g t)"), ALU.subtract
                                      ).then_inc(s["ulo_ok"], 1)
                if do_b:
                    add(b_, c, 1)
                if do_a:
                    dve.wait_ge(d0_in[c % 2], half(a) * (16 * NB))
                    wait(dve, "m_ok", a, -1)
                    decay_scan(c, (0, 1))
                if do_b:
                    add(b_, c, 2)
                if do_c:
                    wait(dve, "ss_ok", z)
                    dve.tensor_scalar(ve[:, :], BG[:, NS + Q:NS + Q + 1], 1.0 / INTER, EPS, ALU.mult, ALU.add
                                      ).then_inc(s["ve_ok"], 1)
                if do_a:
                    decay_scan(c, (2, 3)).then_inc(s["scan_ok"], 1)
                if do_b:
                    add(b_, c, 3)
                if do_a:
                    wait(dve, "xdt_ok", a)
                    wait(dve, "scan_ok", a)
                    wait(dve, "new_ok", a, -1)
                    dve.tensor_tensor(xr[:, :].rearrange("p (h d) -> p h d", d=PD),
                                      xdt[:, :].rearrange("p (h d) -> p h d", d=PD),
                                      lmat[:, :, Q - 1:Q].broadcast_to([P, HEADS, PD]), ALU.mult
                                      ).then_inc(s["xr_ok"], 1)
                if do_b:
                    wait(dve, "yint_ok", b_)
                    wait(dve, "ytr_ok", b_, -1)
                    cp = T["cp_g"][:, :, :, :].rearrange("p t b h -> p (t b h)")[:, bass.ds(times(b_, HEADS), HEADS)]
                    dve.tensor_tensor(y[:, :].rearrange("p (h d) -> p h d", d=PD),
                                      yint[:, :, :].rearrange("p b (h d) -> p (b h) d", d=PD),
                                      cp.unsqueeze(2).broadcast_to([P, HEADS, PD]), ALU.mult).then_inc(s["yi_ok"], 1)
                    wait(dve, "yi_ok", b_)
                    wait(dve, "intra_ok", b_)
                    dve.tensor_tensor(y[:, :], y[:, :], intra[:, :, :, :].rearrange("p b h d -> p (b h d)"),
                                      ALU.add).then_inc(s["y_ok"], 1)
                if do_c:
                    wait(dve, "out_ok", z)
                    wait(dve, "rs_ok", z)
                    xt = x_res[:, :, :].rearrange("p t c -> p (t c)")[:, bass.ds(times(z, HID), HID)]
                    dve.scalar_tensor_tensor(xt, outp[:, :], rstd[:, 0:1], xt, ALU.mult, ALU.add
                                             ).then_inc(s["res_ok"], 1)

            pipeline(dve, step)

        @block.gpsimd
        def _(pool):
            pool.sem_inc(s["smul_ok"], FREE["smul_ok"])
            pool.sem_inc(s["m_ok"], FREE["m_ok"])
            pool.memset(xbd[:, :, :, :], 0.0).then_inc(s["set_ok"], 1)
            for b in range(2):
                pool.memset(bm[b][:, :, :], 0.0).then_inc(s["set_ok"], 1)
            pool.memset(eye_q[:, :], 0.0).then_inc(s["eye_ok"], 1)
            pool.wait_ge(s["eye_ok"], 1)
            for b in range(NB):
                part = eye_q[Q * b:Q * b + Q, :].rearrange("p (h i) -> p h i", i=Q)
                ins = pool.affine_select(out=part, in_=part, compare_op=ALU.not_equal, fill=1.0, base=0,
                                         pattern=[[0, HG], [-1, Q]], channel_multiplier=1)
            ins.then_inc(s["eye_ok"], 1)

            def step(c, i, do_a, do_b, do_c):
                a, b_, z = (i, c), (i, c - 1), (i, c - 2)
                if do_b:
                    pool.wait_ge(dend_in[(c - 1) % 2], half(b_) * 16)
                    for b in range(NB):
                        wait(pool, "add_ok", b_, 0, b) if b else wait(pool, "add_ok", b_, -1)
                        src = s0[(c - 1) % 2][:, :] if b == 0 else s123[:, b - 1, :]
                        pool.tensor_tensor(tmp[:, :].rearrange("p (h d) -> p h d", d=PD),
                                           src.rearrange("p (h d) -> p h d", d=PD),
                                           dend[(c - 1) % 2][:, b, :].unsqueeze(2).broadcast_to([P, HEADS, PD]),
                                           ALU.mult).then_inc(s["smul_ok"], 1)
                if do_c:
                    wait(pool, "ve_ok", z)
                    wait(pool, "res_ok", z, -1)
                    pool.tensor_tensor(rstd[:, :], ve[:, :], T["m_half"][:, 0:1], ALU.pow).then_inc(s["rs_ok"], 1)
                if do_a:
                    wait(pool, "scan_ok", a)
                    wait(pool, "gs_ok", a)
                    wait(pool, "intra_ok", a, -1)
                    pool.tensor_tensor(mmat[:, :, :], lmat[:, :, :],
                                       gs[c % 2][:, :].unsqueeze(1).broadcast_to([P, HEADS, Q]), ALU.mult
                                       ).then_inc(s["m_ok"], 1)

            pipeline(pool, step)

        @block.tensor
        def _(pe):
            for n in ("yint_ok", "new_ok", "intra_ok", "ytr_ok", "ss_ok", "out_ok"):
                pe.sem_inc(s[n], FREE[n])

            def new_state(b_, c, b):
                pe.wait_ge(s["add_ok"], times(b_, NB) + b + 1)
                pe.matmul(new[b % 2][:, :], bm[(c - 1) % 2][:, b, :], xr[:, :], start=True, stop=True
                          ).then_inc(s["new_ok"], 1)

            def intra_heads(heads):
                for hh in heads:
                    for g in range(4):
                        h = HG * g + hh
                        ins = pe.matmul(intra[Q * g:Q * g + Q, :, hh, :], mmat[:, h, :], xbd[:, h, :, :],
                                        start=True, stop=True)
                return ins

            def step(c, i, do_a, do_b, do_c):
                a, b_, z = (i, c), (i, c - 1), (i, c - 2)
                if do_a:
                    wait(pe, "xs_ok", a)
                    wait(pe, "xdt_ok", a, -1)
                    for g in range(4):
                        pe.transpose(X[:, P * g:P * g + P], xT[c % 4][:, g, :], T["ident"][:, :])
                    wait(pe, "bc_ok", a)
                    wait(pe, "bm_ok", a, -1)
                    wait(pe, "gs_ok", a, -1)
                    wait(pe, "ve_ok", a, -3)
                    pe.transpose(BG[:, 0:NS], bc[c % 4][:, 0, :], T["ident"][:, :])
                    for b in range(NB):
                        r = slice(Q * b, Q * b + Q)
                        ins = pe.matmul(BG[r, NS:NS + Q], bc[c % 4][:, 0, r], bc[c % 4][:, 1, r], start=True, stop=True)
                    ins.then_inc(s["tr_ok"], 1)
                if do_c:
                    wait(pe, "y_ok", z)
                    wait(pe, "yf_ok", z, -1)
                    for b in range(NB):
                        ins = pe.transpose(ytr[:, b, :], y[:, P * b:P * b + P], T["ident"][:, :])
                    ins.then_inc(s["ytr_ok"], 1)
                if do_b:
                    wait(pe, "xr_ok", b_)
                    wait(pe, "bm_ok", b_)
                    new_state(b_, c, 0)
                    new_state(b_, c, 1)
                    wait(pe, "m_ok", b_)
                    wait(pe, "xbd_ok", b_)
                    wait(pe, "y_ok", b_, -1)
                    intra_heads(range(0, 4))
                    new_state(b_, c, 2)
                    intra_heads(range(4, 8))
                if do_c:
                    wait(pe, "red_ok", z)
                    if do_a:
                        wait(pe, "bm_ok", a)
                    pe.matmul(BG[:, NS + Q:NS + Q + 1], ssum[:, :], T["ones"][:, 0:1], start=True, stop=True
                              ).then_inc(s["ss_ok"], 1)
                if do_b:
                    new_state(b_, c, 3)
                    intra_heads(range(8, HG)).then_inc(s["intra_ok"], 1)
                    for b in range(NB):
                        wait(pe, "add_ok", b_, 0, b) if b else wait(pe, "add_ok", b_, -1)
                        st = s0[(c - 1) % 2] if b == 0 else s123[:, b - 1, :]
                        for g in range(4):
                            ins = pe.matmul(yint[Q * g:Q * g + Q, b, :], bc[(c - 1) % 4][:, 1, Q * b:Q * b + Q],
                                            st[:, P * g:P * g + P], start=True, stop=True)
                    ins.then_inc(s["yint_ok"], 1)
                if do_c:
                    wait(pe, "ulo_ok", z)
                    wait(pe, "res_ok", z, -1)
                    for k in range(4):
                        ins = split_mm(pe, outp[:, :], uh[:, 0, k, :], uh[:, 1, k, :], wout[:, 0, k, :],
                                       wout[:, 1, k, :], k == 0, k == 3)
                    ins.then_inc(s["out_ok"], 1)

            pipeline(pe, step)


def build(nc, A, out):
    T = {}
    for name, shape, dt in (("a_dram", (BLOCKS, HEADS, Q), F32), ("dend_dram", (BLOCKS, HEADS), F32),
                            ("wgu_dram", (P, 2, KC, GUC, P), F32), ("wd_dram", (P, 2, FCH, HID), F32)):
        T[name] = nc.dram_tensor(name, shape, dt, kind="Internal").ap()
    with ExitStack() as base:
        def put(stack, *tensors, side="left"):
            for name, shape, *dt in tensors:
                T[name] = stack.enter_context(nc.sbuf_tensor(f"{name}_{len(T)}", shape, (dt or [F32])[0], side=side))

        put(base, ("x_res", [P, TILES, HID]), ("wout", [P, 2, 4, HID], F32R), ("ident", [P, P]), ("ones", [P, 1]),
            ("m_half", [P, GT]), ("norm_w", [P, 4]), ("conv_b", [P, XCH]), ("conv_w", [P, XCH, KCONV]),
            ("a_log", [P, 1]), ("dt_b", [P, 1]), ("d_ch", [P, 4]))
        ffn_w = (("wgu", [P, 2, KC, GUC, P], F32R), ("wd", [P, 2, FCH, HID], F32R))
        with ExitStack() as win_s:
            norm = Norm(nc, win_s, T, "n1_", side="right")
            put(win_s, ("win", [P, 2, KC, PCH, P], F32R), side="right")
            with ExitStack() as ffn1:
                put(ffn1, *ffn_w)
                build_weights(nc, T, A, norm)
                build_ffn(nc, T, "f1_", norm)
            mamba = ExitStack()
            put(mamba, ("cv", [P, XCH, L]), ("zs", [P, 4, L]), ("dt_tok", [P, TILES, HEADS]),
                ("cp_g", [P, TILES, NB, HG]))
            raw = ExitStack()
            put(raw, ("dt_raw", [P, L]))
            build_in_proj(nc, T, norm)
        build_decay(nc, T)
        raw.close()
        build_scan(nc, T)
        mamba.close()
        with ExitStack() as ffn2:
            for name, shape, dt in ffn_w:
                ffn2.enter_context(nc.sbuf_tensor(name + "_again", shape, dt))
            build_ffn(nc, T, "f2_", Norm(nc, ffn2, T, "n2_"), out)


_INS = dict(x="L0_attn_hidden_states", in_w="L0_attn_in_proj_w", conv_w="L0_attn_conv_w", conv_b="L0_attn_conv_b",
            A_log="L0_attn_A_log", D="L0_attn_D", dt_bias="L0_attn_dt_bias", norm_w="L0_attn_norm_w",
            out_w="L0_attn_out_proj_w", lut="L0_ffn_lut", gate="L0_ffn_gate_idx", up="L0_ffn_up_idx",
            down="L0_ffn_down_idx")


def kernel(**inputs):
    import numpy as _np
    import concourse.bacc as _bacc
    from concourse.bass_utils import run_bass_kernel_spmd as _run

    nc = _bacc.Bacc("TRN2", target_bir_lowering=False, num_devices=1)
    arrays, args = {}, {}
    for short, name in _INS.items():
        a = _np.ascontiguousarray(inputs[name])
        arrays[f"in_{short}"] = a
        args[short] = nc.dram_tensor(f"in_{short}", a.shape, mybir.dt.from_np(a.dtype), kind="ExternalInput").ap()
    out = nc.dram_tensor("out_0", (1, L, HID), F32, kind="ExternalOutput").ap()
    build(nc, args, out)
    return _run(nc, [arrays], core_ids=[0]).results[0]["out_0"]
```

```python
from contextlib import ExitStack

import concourse.bass as bass
from concourse import mybir

F32 = mybir.dt.float32
F32R = mybir.dt.float32r
I32 = mybir.dt.int32
ALU = mybir.AluOpType
ACT = mybir.ActivationFunctionType

P = 128
L = 2048
HID = 256
KC = HID // P
TILES = L // P
GT = 4
GROUPS = TILES // GT
GN = GT * P
FF = 688
FCH = 6
FLAST = FF - 5 * P
LUT = 16
INTER = 512
HEADS = 64
PD = INTER // HEADS
NS = 128
KCONV = 4
CONV = INTER + 2 * NS
PROJ = 2 * INTER + 2 * NS + HEADS
PCH = 11
XCH = CONV // P
Q = 32
NB = P // Q
BLOCKS = L // Q
HG = 16
EPS = 1e-5
MUP_Z, MUP_X = 0.25, 0.5
GUC = 11


def split_mm(pe, out, w_hi, w_lo, x_hi, x_lo, start, stop):
    pe.matmul(out, w_hi, x_hi, start=start, stop=False)
    pe.matmul(out, w_hi, x_lo, start=False, stop=False)
    return pe.matmul(out, w_lo, x_hi, start=False, stop=stop)


def build_weights(nc, T, A, norm):
    with ExitStack() as ctx:
        sb = lambda n, s, d=F32: ctx.enter_context(nc.sbuf_tensor(n, s, d))
        sem = lambda n: ctx.enter_context(nc.semaphore(n))
        gu_idx = sb("gu_idx", [P, GUC, HID], I32)
        dn_idx = sb("dn_idx", [P, 2, FF], I32)
        mask = [sb(f"mask{b}", [P, LUT, HID], F32R) for b in range(2)]
        lut = sb("lut_bc", [P, LUT])
        lut_h, lut_l = sb("lut_h", [P, LUT], F32R), sb("lut_l", [P, LUT], F32R)
        diag = sb("diag", [P, LUT, 2, P], F32R)
        win_raw = sb("win_raw", [P, KC, PROJ])
        wout_raw = sb("wout_raw", [P, 4, HID])
        bank = [ctx.enter_context(nc.psum_tensor(f"look{b}", [P, 2, 2, P], F32)) for b in range(2)]
        idx_pad, gate_in, up_in, mix_in, down_in, lut_in, x_in, small_in, win_in, wout_in = map(sem, (
            "idx_pad", "gate_in", "up_in", "mix_in", "down_in", "lut_in", "x_in", "small_in", "win_in", "wout_in"))
        lut_ok, diag_ok, mask_ok, prod_ok, evac_ok, zeroed, split_hi, wout_s, split_lo, ident_ok = map(sem, (
            "lut_ok", "diag_ok", "mask_ok", "prod_ok", "evac_ok", "zeroed", "split_hi", "wout_s", "split_lo",
            "ident_ok"))
        win, wout, wgu, wd = T["win"], T["wout"], T["wgu"], T["wd"]
        DOWN = [(m, 2 * P * j, min(2 * P, FF - 2 * P * j), [(f, min(P, FF - P * f)) for f in (2 * j, 2 * j + 1)])
                for m in range(2) for j in range(FCH // 2)]
        x0_in, half_ok, *first_in = map(sem, ("x0_in", "half_ok", "first_in0", "first_in1"))
        x_in_dram = A["x"][0].rearrange("(t p) c -> p t c", p=P)
        block = ctx.enter_context(nc.Block())

        @block.sync
        def _(sp):
            sp.dma_start(lut[:, :], A["lut"].unsqueeze(0).broadcast_to([P, LUT])).then_inc(lut_in, 16)
            for c in range(2):
                sp.dma_start(gu_idx[:, c, :], A["gate"][c * P:c * P + P, :]).then_inc(first_in[c], 16)
            sp.dma_start(gu_idx[:, 2:5, :], A["gate"][2 * P:5 * P, :].rearrange("(c p) h -> p c h", p=P)
                         ).then_inc(gate_in, 16)
            sp.dma_start(T["x_res"][:, 0:GT, :], x_in_dram[:, 0:GT, :]).then_inc(x0_in, 16)
            sp.wait_ge(idx_pad, 1)
            sp.dma_start(gu_idx[0:FLAST, 10, :], A["gate"][5 * P:FF, :]).then_inc(mix_in, 16)
            sp.dma_start(gu_idx[64:64 + FLAST, 10, :], A["up"][5 * P:FF, :]).then_inc(mix_in, 16)
            sp.dma_start(dn_idx[:, :, :], A["down"].rearrange("(c p) f -> p c f", p=P)).then_inc(down_in, 16)
            sp.dma_start(win_raw[:, :, :], A["in_w"].rearrange("(k p) n -> p k n", p=P)).then_inc(win_in, 16)
            sp.dma_start(T["x_res"][:, GT:, :], x_in_dram[:, GT:, :]).then_inc(x_in, 16)
            sp.dma_start(wout_raw[:, :, :], A["out_w"].rearrange("(k p) n -> p k n", p=P)).then_inc(wout_in, 16)
            with nc.allow_non_contiguous_dma(reason="per-channel vectors, small"):
                sp.dma_start(T["norm_w"][:, :], A["norm_w"].rearrange("(k p) -> p k", p=P)).then_inc(small_in, 16)
                sp.dma_start(T["conv_b"][:, :], A["conv_b"].rearrange("(k p) -> p k", p=P)).then_inc(small_in, 16)
                sp.dma_start(T["conv_w"][:, :, :], A["conv_w"].rearrange("(k p) j -> p k j", p=P)
                             ).then_inc(small_in, 16)
                for half in range(2):
                    r = slice(HEADS * half, HEADS * half + HEADS)
                    sp.dma_start(T["a_log"][r, :], A["A_log"].unsqueeze(1)).then_inc(small_in, 16)
                    sp.dma_start(T["dt_b"][r, :], A["dt_bias"].unsqueeze(1)).then_inc(small_in, 16)
                for hh in range(HG):
                    sp.dma_start(T["d_ch"][PD * hh:PD * hh + PD, :],
                                 A["D"].rearrange("(g h) -> h g", h=HG)[hh:hh + 1, :].broadcast_to([PD, 4])
                                 ).then_inc(small_in, 16)
            sp.wait_ge(x_in, 16)
            sp.wait_ge(small_in, 16 * (7 + HG))

        @block.gpsimd
        def _(pool):
            pool.memset(T["ident"][:, :], 0.0).then_inc(ident_ok, 1)
            pool.wait_ge(ident_ok, 1)
            pool.affine_select(out=T["ident"][:, :], in_=T["ident"][:, :], compare_op=ALU.not_equal, fill=1.0,
                               base=0, pattern=[[-1, P]], channel_multiplier=1).then_inc(ident_ok, 1)
            pool.memset(gu_idx[:, GUC - 1, :], LUT).then_inc(idx_pad, 1)
            pool.memset(T["ones"][:, :], 1.0)
            pool.memset(T["m_half"][:, :], -0.5).then_inc(half_ok, 1)
            for hl in range(2):
                pool.memset(wd[:, hl, FCH - 1, :].bitcast(F32), 0.0).then_inc(zeroed, 1)
            pool.wait_ge(half_ok, 1)
            norm.pool_rstd(pool, 0)
            pool.wait_ge(split_hi, 2)
            pool.tensor_tensor(win[:, 1, :, :, :].rearrange("p k c n -> p k (c n)")[:, :, 0:PROJ], win_raw[:, :, :],
                               win[:, 0, :, :, :].rearrange("p k c n -> p k (c n)")[:, :, 0:PROJ].bitcast(F32),
                               ALU.subtract)
            pool.tensor_tensor(win[:, 1, :, PCH - 1, HEADS:P], win_raw[:, :, PROJ - HEADS:PROJ],
                               win[:, 0, :, PCH - 1, HEADS:P].bitcast(F32), ALU.subtract)
            pool.wait_ge(split_hi, 3)
            pool.tensor_tensor(wout[:, 1, :, :], wout_raw[:, :, :], wout[:, 0, :, :].bitcast(F32), ALU.subtract)

        @block.vector
        def _(dve):
            dve.wait_ge(lut_in, 16)
            dve.tensor_copy(lut_h[:, :], lut[:, :]).then_inc(lut_ok, 1)
            dve.wait_ge(lut_ok, 1)
            dve.tensor_tensor(lut_l[:, :], lut[:, :], lut_h[:, :].bitcast(F32), ALU.subtract).then_inc(lut_ok, 1)
            dve.wait_ge(lut_ok, 2)
            dve.wait_ge(ident_ok, 2)
            dve.wait_ge(first_in[0], 16)
            for k in range(LUT):
                for hl, part in enumerate((lut_h, lut_l)):
                    dve.tensor_scalar(diag[:, k, hl, :], T["ident"][:, :], part[:, k:k + 1].bitcast(F32), None,
                                      ALU.mult).then_inc(diag_ok, 1)
                dve.tensor_scalar(mask[0][:, k, :], gu_idx[:, 0, :], float(k), None, ALU.is_equal
                                  ).then_inc(mask_ok, 1)

            def masks(b, src, n, unit):
                dve.wait_ge(prod_ok, unit + 1)
                for k in range(LUT):
                    dve.tensor_scalar(mask[b][:, k, 0:n], src, float(k), None, ALU.is_equal).then_inc(mask_ok, 1)

            dve.sem_inc(prod_ok, 2)
            gu = gu_idx[:, :, :].rearrange("p c h -> p (c h)")
            dve.wait_ge(first_in[1], 16)
            masks(1, gu_idx[:, 1, :], HID, 1)
            dve.wait_ge(gate_in, 16)
            dve.wait_ge(up_in, 16)
            dve.wait_ge(x0_in, 16)
            norm.dve_start(dve)
            norm.dve_stats(dve, 0)
            norm.dve_xn(dve, 0)
            with dve.Fori(1, GUC // 2) as i:
                for b in range(2):
                    masks(b, gu[:, bass.ds(i * (2 * HID) + b * HID, HID)], HID, i * 2 + b)
            dve.wait_ge(mix_in, 32)
            masks(0, gu_idx[:, GUC - 1, :], HID, GUC - 1)
            dve.wait_ge(down_in, 16)
            for n, (m, f0, cols, _) in enumerate(DOWN):
                masks((GUC + n) % 2, dn_idx[:, m, f0:f0 + cols], cols, GUC + n)
            norm.dve_lo(dve, 0)

        @block.scalar
        def _(act):
            act.dma_start(gu_idx[:, 5:10, :], A["up"][0:5 * P, :].rearrange("(c p) h -> p c h", p=P)
                          ).then_inc(up_in, 16)
            def win_hi():
                act.wait_ge(win_in, 16)
                act.activation(win[:, 0, :, :, :].rearrange("p k c n -> p k (c n)")[:, :, 0:PROJ], win_raw[:, :, :],
                               ACT.Copy).then_inc(split_hi, 1)
                act.activation(win[:, 0, :, PCH - 1, HEADS:P], win_raw[:, :, PROJ - HEADS:PROJ], ACT.Copy
                               ).then_inc(split_hi, 1)

            act.sem_inc(evac_ok, 2)

            def evac(b, unit, squares):
                act.wait_ge(prod_ok, unit + 3)
                for n, (dst, rows) in enumerate(squares):
                    ins = act.activation(dst, bank[b][0:rows, n, :, :], ACT.Copy)
                ins.then_inc(evac_ok, 1)

            gu = wgu[:, :, :, :, :].rearrange("p l k c n -> p l k (c n)")
            for unit in range(2):
                evac(unit, unit, [(wgu[:, :, kc, unit, :], P) for kc in range(KC)])
            norm.act_hi(act, 0)
            win_hi()
            with act.Fori(1, GUC // 2) as i:
                for b in range(2):
                    cols = bass.ds(i * (2 * P) + b * P, P)
                    evac(b, i * 2 + b, [(gu[:, :, kc, cols], P) for kc in range(KC)])
            act.wait_ge(wout_in, 16)
            act.wait_ge(small_in, 16 * (7 + HG))
            for k in range(4):
                act.activation(wout_raw[:, k, :], wout_raw[:, k, :], ACT.Copy,
                               scale=T["norm_w"][:, k:k + 1]).then_inc(wout_s, 1)
            act.wait_ge(wout_s, 4)
            act.activation(wout[:, 0, :, :], wout_raw[:, :, :], ACT.Copy).then_inc(split_hi, 1)
            evac(0, GUC - 1, [(wgu[:, :, kc, GUC - 1, :], P) for kc in range(KC)])
            act.wait_ge(zeroed, 2)
            for n, (m, _, _, fs) in enumerate(DOWN):
                evac((GUC + n) % 2, GUC + n, [(wd[0:rows, :, f, P * m:P * m + P], rows) for f, rows in fs])

        @block.tensor
        def _(pe):
            def lookup(b, unit):
                pe.wait_ge(evac_ok, unit + 1)
                for n in range(2):
                    for k in range(LUT):
                        if n == 0 and k % 4 == 0:
                            pe.wait_ge(mask_ok, unit * LUT + k + 4)
                            if isinstance(unit, int) and unit == 0:
                                pe.wait_ge(diag_ok, 2 * (k + 4))
                        ins = pe.matmul(bank[b][:, n, :, :], mask[b][:, k, P * n:P * n + P], diag[:, k, :, :],
                                        start=k == 0, stop=k == LUT - 1)
                ins.then_inc(prod_ok, 1)

            for unit in range(2):
                lookup(unit, unit)
            norm.pe_transpose(pe, 0)
            with pe.Fori(1, GUC // 2) as i:
                for b in range(2):
                    lookup(b, i * 2 + b)
            for unit in range(GUC - 1, GUC + len(DOWN)):
                lookup(unit % 2, unit)


class Norm:

    def __init__(self, nc, ctx, T, tag, side="left"):
        sb = lambda n, s, d=F32: ctx.enter_context(nc.sbuf_tensor(tag + n, s, d, side=side))
        sem = lambda n: ctx.enter_context(nc.semaphore(tag + n))
        self.T = T
        self.stats = sb("stats", [P, GT, 6])
        self.mv = sb("mv", [P, GT, 2])
        self.ve = sb("ve", [P, GT])
        self.rstd = sb("rstd", [P, GT])
        self.xn = sb("xn", [P, GT, HID])
        self.xT = sb("xT", [P, 2, KC, L], F32R)
        self.base = 0
        self.pt = [ctx.enter_context(nc.psum_tensor(f"{tag}pt{k}", [P, GN], F32)) for k in range(KC)]
        self.stat_ok, self.mv_ok, self.ve_ok, self.rstd_ok = map(sem, ("stat_ok", "mv_ok", "ve_ok", "rstd_ok"))
        self.xn_ok, self.pt_ok, self.hi_ok, self.lo_ok = map(sem, ("xn_ok", "pt_ok", "hi_ok", "lo_ok"))
        self.stat_seen = sem("stat_seen")

    def rows(self, g, t):
        g = g % GROUPS if isinstance(g, int) else g
        x = self.T["x_res"][:, :, :].rearrange("p t c -> p (t c)")
        return x[:, bass.ds(g * (GT * HID) + t * HID, HID)]

    def tokens(self, g):
        return bass.ds((g % GROUPS if isinstance(g, int) else g) * GN, GN)

    def dve_start(self, dve):
        dve.sem_inc(self.lo_ok, KC)
        dve.sem_inc(self.pt_ok, 1)

    def dve_stats(self, dve, g):
        for t in range(GT):
            dve.bn_stats(self.stats[:, t, :], self.rows(g, t)).then_inc(self.stat_ok, 1)
        dve.wait_ge(self.stat_ok, (g + self.base) * GT + GT)
        dve.sem_inc(self.stat_seen, 1)
        for t in range(GT):
            dve.bn_aggr(self.mv[:, t, :], self.stats[:, t, :]).then_inc(self.mv_ok, 1)
        dve.wait_ge(self.mv_ok, (g + self.base) * GT + GT)
        dve.tensor_scalar(self.ve[:, :], self.mv[:, :, 1], EPS, None, ALU.add).then_inc(self.ve_ok, 1)

    def pool_rstd(self, pool, g):
        pool.wait_ge(self.ve_ok, g + self.base + 1)
        pool.tensor_tensor(self.rstd[:, :], self.ve[:, :], self.T["m_half"][:, 0:GT], ALU.pow).then_inc(self.rstd_ok, 1)

    def dve_xn(self, dve, g):
        dve.wait_ge(self.rstd_ok, g + self.base + 1)
        dve.wait_ge(self.pt_ok, g + self.base + 1)
        for t in range(GT):
            dve.tensor_scalar(self.xn[:, t, :], self.rows(g, t), self.mv[:, t, 0:1], self.rstd[:, t:t + 1],
                              ALU.subtract, ALU.mult).then_inc(self.xn_ok, 1)

    def pe_transpose(self, pe, g):
        pe.wait_ge(self.xn_ok, (g + self.base) * GT + GT)
        pe.wait_ge(self.lo_ok, (g + self.base) * KC + KC)
        for kc in range(KC):
            for t in range(GT):
                last = pe.transpose(self.pt[kc][:, P * t:P * t + P], self.xn[:, t, P * kc:P * kc + P],
                                    self.T["ident"][:, :])
        last.then_inc(self.pt_ok, 1)

    def act_hi(self, act, g):
        act.wait_ge(self.pt_ok, g + self.base + 2)
        for kc in range(KC):
            act.activation(self.xT[:, 0, kc, self.tokens(g)], self.pt[kc][:, :], ACT.Copy).then_inc(self.hi_ok, 1)

    def dve_lo(self, dve, g):
        for kc in range(KC):
            dve.wait_ge(self.hi_ok, (g + self.base) * KC + kc + 1)
            dve.tensor_tensor(self.xT[:, 1, kc, self.tokens(g)], self.pt[kc][:, :], self.xT[:, 0, kc, self.tokens(g)].bitcast(F32),
                              ALU.subtract).then_inc(self.lo_ok, 1)

    def pe_ready(self, pe, g, kc):
        pe.wait_ge(self.lo_ok, (g + self.base) * KC + kc + 1 + KC)


def over_groups(eng, body, last_too=False):
    with eng.Fori(0, GROUPS - 1) as g:
        body(g, True)
    body(GROUPS - 1, last_too)


def build_ffn(nc, T, tag, norm, out=None):
    with ExitStack() as ctx:
        sb = lambda n, s, d=F32: ctx.enter_context(nc.sbuf_tensor(tag + n, s, d))
        ps = lambda n, s: ctx.enter_context(nc.psum_tensor(tag + n, s, F32))
        sem = lambda n: ctx.enter_context(nc.semaphore(tag + n))
        first = out is None
        hT = sb("hT", [P, 2, FCH, GN], F32R)
        sg = [sb(f"sg{b}", [P, GN]) for b in range(2)]
        h = sb("h", [P, GN])
        gate = [ps(f"gate{b}", [P, GN]) for b in range(2)]
        up = [ps(f"up{b}", [P, GN]) for b in range(2)]
        down = [ps(f"down{b}", [P, 2, HID]) for b in range(2)]
        gate_ok, up_ok, silu_ok, h_ok, h_hi, h_lo = map(sem, ("gate_ok", "up_ok", "silu_ok", "h_ok", "h_hi", "h_lo"))
        down_ok, res_ok, hz, stored = map(sem, ("down_ok", "res_ok", "hz", "stored"))
        wgu, wd, x_res = T["wgu"], T["wd"], T["x_res"]
        xflat = x_res[:, :, :].rearrange("p t c -> p (t c)")
        PAIRS = GT // 2
        block = ctx.enter_context(nc.Block())

        def rows(c):
            return P if c < FCH - 1 else FLAST

        @block.vector
        def _(dve):
            dve.sem_inc(h_ok, 2)
            if not first:
                norm.dve_start(dve)
                norm.dve_stats(dve, 0)
                norm.dve_xn(dve, 0)
                norm.dve_lo(dve, 0)

            def body(g, ahead):
                for c in range(FCH):
                    r = rows(c)
                    dve.wait_ge(silu_ok, g * FCH + c + 1)
                    if c < FCH - 1:
                        dve.wait_ge(up_ok, g * (FCH - 1) + c + 1)
                        other = up[c % 2][:, :]
                    else:
                        other = gate[c % 2][64:64 + r, :]
                    dve.tensor_tensor(h[0:r, :], sg[c % 2][0:r, :], other, ALU.mult).then_inc(h_ok, 1)
                    dve.wait_ge(h_hi, g * FCH + c + 1)
                    dve.tensor_tensor(hT[0:r, 1, c, :], h[0:r, :], hT[0:r, 0, c, :].bitcast(F32),
                                      ALU.subtract).then_inc(h_lo, 1)
                    if ahead and c == 0:
                        norm.dve_stats(dve, g + 1)
                    if ahead and c == 2:
                        norm.dve_xn(dve, g + 1)
                    dve.wait_ge(h_lo, g * FCH + c + 1)
                if ahead:
                    norm.dve_lo(dve, g + 1)
                for j in range(PAIRS):
                    dve.wait_ge(down_ok, g * PAIRS + j + 1)
                    xt = xflat[:, bass.ds(g * (GT * HID) + j * (2 * HID), 2 * HID)]
                    dve.scalar_tensor_tensor(xt, down[j][:, :, :].rearrange("p t c -> p (t c)"), 0.5, xt,
                                             ALU.mult, ALU.add).then_inc(res_ok, 1)

            over_groups(dve, body, first)

        @block.gpsimd
        def _(pool):
            pool.memset(hT[:, 0, FCH - 1, :].bitcast(F32), 0.0).then_inc(hz, 1)
            pool.memset(hT[:, 1, FCH - 1, :].bitcast(F32), 0.0).then_inc(hz, 1)
            if not first:
                norm.pool_rstd(pool, 0)
            with pool.Fori(0, GROUPS - 1) as g:
                norm.pool_rstd(pool, g + 1)
            if first:
                norm.pool_rstd(pool, GROUPS)

        @block.scalar
        def _(act):
            act.wait_ge(hz, 2)
            if not first:
                norm.act_hi(act, 0)

            def body(g, ahead):
                for c in range(FCH):
                    r = rows(c)
                    act.wait_ge(gate_ok, g * FCH + c + 1)
                    act.activation(sg[c % 2][0:r, :], gate[c % 2][0:r, :], ACT.Silu).then_inc(silu_ok, 1)
                    act.wait_ge(h_ok, g * FCH + c + 3)
                    act.activation(hT[0:r, 0, c, :], h[0:r, :], ACT.Copy).then_inc(h_hi, 1)
                if ahead:
                    norm.act_hi(act, g + 1)

            over_groups(act, body, first)

        @block.tensor
        def _(pe):
            pe.sem_inc(res_ok, PAIRS)
            pe.wait_ge(hz, 2)
            if not first:
                norm.pe_transpose(pe, 0)
            x_hi, x_lo = norm.xT[:, 0], norm.xT[:, 1]

            def body(g, ahead):
                for c in range(FCH):
                    pe.wait_ge(h_ok, g * FCH + c + 1)
                    parts = [(gate[c % 2], c, gate_ok), (up[c % 2], 5 + c, up_ok)] if c < FCH - 1 \
                        else [(gate[c % 2], GUC - 1, gate_ok)]
                    for bank, wc, done in parts:
                        for kc in range(KC):
                            if wc == 0:
                                norm.pe_ready(pe, g, kc)
                            last = split_mm(pe, bank[:, :], wgu[:, 0, kc, wc, :], wgu[:, 1, kc, wc, :],
                                            x_hi[:, kc, norm.tokens(g)], x_lo[:, kc, norm.tokens(g)],
                                            kc == 0, kc == KC - 1)
                        last.then_inc(done, 1)
                if ahead:
                    norm.pe_transpose(pe, g + 1)
                LASTC = (FCH - 1,)
                parts = ((0, 0, range(FCH - 1)), (1, 0, range(FCH - 1)), (0, 0, LASTC), (0, 1, range(FCH)),
                         (1, 0, LASTC), (1, 1, range(FCH)))
                for n, (j, t, chunks) in enumerate(parts):
                    if n < PAIRS:
                        pe.wait_ge(res_ok, g * PAIRS + j + 1)
                    tok = slice(P * (2 * j + t), P * (2 * j + t) + P)
                    for c in chunks:
                        if n == 0 or n == 2:
                            pe.wait_ge(h_lo, g * FCH + c + 1)
                        last = split_mm(pe, down[j][:, t, :], hT[:, 0, c, tok], hT[:, 1, c, tok],
                                        wd[:, 0, c, :], wd[:, 1, c, :], c == 0, c == FCH - 1)
                    if t:
                        last.then_inc(down_ok, 1)

            over_groups(pe, body, first)

        @block.sync
        def _(sp):
            if out is None:
                for name in ("wgu", "wd"):
                    chip = T[name][tuple([slice(None)] * len(T[name].shape))].bitcast(F32)
                    sp.dma_start(T[name + "_dram"], chip).then_inc(stored, 16)
                sp.wait_ge(stored, 32)
            else:
                dst = out[0].rearrange("(t p) c -> p t c", p=P)
                for g in range(GROUPS):
                    sp.wait_ge(res_ok, (g + 2) * PAIRS)
                    sp.dma_start(dst[:, g * GT:g * GT + GT, :], x_res[:, g * GT:g * GT + GT, :]).then_inc(stored, 16)
                sp.wait_ge(stored, 16 * GROUPS)


def build_in_proj(nc, T, norm):
    with ExitStack() as ctx:
        sb = lambda n, s, d=F32: ctx.enter_context(nc.sbuf_tensor(n, s, d))
        sem = lambda n: ctx.enter_context(nc.semaphore(n))
        norm.base = GROUPS
        HALO = KCONV - 1
        pre = sb("pre", [P, XCH, HALO + GN])
        prod = sb("prod", [P, GN])
        first = sb("first", [P, 2, GN])
        bank = [ctx.enter_context(nc.psum_tensor(f"pj{b}", [P, GN], F32)) for b in range(4)]
        mm_ok, ev_ok, carry_v, carry_p, tap_v, tap_p = map(sem, ("mm_ok", "ev_ok", "carry_v", "carry_p", "tap_v", "tap_p"))
        w_ok, prod_ok, seen, pre_ok, first_ok = map(sem, ("w_ok", "prod_ok", "seen", "pre_ok", "first_ok"))
        win, cv, zs = T["win"], T["cv"], T["zs"]
        cw, cb = T["conv_w"], T["conv_b"]
        H = GN // 2
        HB = H // Q
        HT = H // P
        raw, e, u, ln, dt, a, a0, cp = (sb(n, [P, H]) for n in ("raw", "e_abs", "one_e", "ln_u", "dtT", "aT", "a0T",
                                                                "cpT"))
        A, eA = sb("A_neg", [P, 1]), sb("eA", [P, 1])
        dend, dendT = sb("dend", [P, HB]), sb("dendT", [HB, P])
        pt_dt = ctx.enter_context(nc.psum_tensor("pt_dt", [P, HT, P], F32))
        pt_cp = ctx.enter_context(nc.psum_tensor("pt_cp", [P, HT + 1, P], F32))
        eA_ok, A_ok, zero_ok, raw_ok, abs_ok, exp_ok, ln_ok, a_ok, dttok_ok = map(sem, (
            "eA_ok", "A_ok", "zero_ok", "raw_ok", "abs_ok", "exp_ok", "ln_ok", "a_ok", "dttok_ok"))
        u_ok, nd_ok, s_ok, dt_ok, a0_ok, az_ok, cp_ok, dend_ok, dendT_ok, cpg_ok, tr_dt, tr_cp = map(sem, (
            "u_ok", "nd_ok", "s_ok", "dt_ok", "a0_ok", "az_ok", "cp_ok", "dend_ok", "dendT_ok", "cpg_ok", "tr_dt",
            "tr_cp"))
        a_sent, dend_sent = map(sem, ("a_sent", "dend_sent"))
        halves = [(k, slice(HEADS * k, HEADS * k + HEADS)) for k in range(2)]
        done = lambda g: g + 2
        ORDER = (4, 8, 10, 5, 6, 9, 7, 0, 1, 2, 3)
        V_CH, P_CH = (0, 1, 2, 3), (4, 5)
        EV_FREE = 3
        block = ctx.enter_context(nc.Block())

        def evacuated(g, place):
            return g * PCH + (place + 1 + EV_FREE)

        @block.vector
        def _(dve):
            dve.tensor_scalar(cw[:, :, :], cw[:, :, :], MUP_X, None, ALU.mult).then_inc(w_ok, 1)
            dve.memset(pre[:, 0:len(V_CH), 0:HALO], 0.0).then_inc(carry_v, len(V_CH))
            dve.wait_ge(w_ok, 1)
            dve.sem_inc(dt_ok, 1)
            dve.sem_inc(cp_ok, 1)
            dve.sem_inc(cpg_ok, 1)
            dve.wait_ge(eA_ok, 1)
            dve.tensor_scalar(A[:, :], eA[:, :], -1.0, None, ALU.mult).then_inc(A_ok, 1)
            dve.wait_ge(zero_ok, 1)

            def one_plus_e(g):
                dve.wait_ge(exp_ok, g + 1)
                dve.tensor_scalar(u[:, :], e[:, :], 1.0, None, ALU.add).then_inc(u_ok, 1)
                dve.wait_ge(u_ok, g + 1)
                dve.scalar_tensor_tensor(e[:, :], u[:, :], 1.0, e[:, :], ALU.subtract, ALU.subtract
                                         ).then_inc(nd_ok, 1)

            def softplus(g):
                dve.wait_ge(nd_ok, g + 1)
                dve.wait_ge(ln_ok, g + 1)
                dve.tensor_tensor(ln[:, :], ln[:, :], e[:, :], ALU.subtract).then_inc(s_ok, 1)
                dve.wait_ge(s_ok, g + 1)
                dve.wait_ge(a_ok, done(g - 1))
                dve.wait_ge(tr_dt, done(g - 1))
                dve.scalar_tensor_tensor(dt[:, :], raw[:, :], 0.0, ln[:, :], ALU.max, ALU.add).then_inc(dt_ok, 1)

            def products(g):
                dve.wait_ge(a_ok, done(g))
                dve.tensor_copy(a0[:, 0:H:Q], a[:, 0:H:Q]).then_inc(a0_ok, 1)
                dve.wait_ge(a0_ok, g + 1)
                dve.memset(a[:, 0:H:Q], 0.0).then_inc(az_ok, 1)
                dve.wait_ge(az_ok, g + 1)
                dve.wait_ge(tr_cp, done(g - 1))
                dve.tensor_tensor_scan(cp[:, :], a[:, :], a0[:, :], 0.0, ALU.mult, ALU.add).then_inc(cp_ok, 1)
                dve.wait_ge(cp_ok, done(g))
                dve.tensor_copy(dend[:, :], cp[:, Q - 1:H:Q]).then_inc(dend_ok, 1)

            def by_token(g):
                dve.wait_ge(tr_cp, done(g))
                dve.wait_ge(dend_sent, g * 16 + 16)
                dve.tensor_copy(dendT[:, :], pt_cp[0:HB, HT, :]).then_inc(dendT_ok, 1)
                cols = T["cp_g"][:, :, :, :].rearrange("p t b h -> p (t b h)")[:, bass.ds(g * (GT * HEADS), GT * HEADS)]
                cols = cols.rearrange("p (t b h) -> p t b h", b=NB, h=HG)
                for b in range(NB):
                    for q in range(4):
                        ins = dve.tensor_copy(
                            cols[Q * q:Q * q + Q, :, b, :].rearrange("p (k t) h -> p k t h", k=2),
                            pt_cp[Q * b:Q * b + Q, 0:HT, :].rearrange("p t (k h) -> p k t h", k=2)
                            [:, :, :, HG * q:HG * q + HG])
                ins.then_inc(cpg_ok, 1)

            def body(g, ahead):
                if ahead:
                    norm.dve_stats(dve, g + 1)
                n = 0
                for c in V_CH:
                    dve.wait_ge(ev_ok, evacuated(g, ORDER.index(4 + c)))
                    dst = cv[:, c, bass.ds(g * GN, GN)]
                    for k in range(HALO):
                        if k:
                            dve.wait_ge(tap_v, g * (HALO * len(V_CH)) + n)
                        dve.scalar_tensor_tensor(dst, pre[:, c, k:k + GN], cw[:, c, k:k + 1], dst,
                                                 ALU.mult, ALU.add).then_inc(tap_v, 1)
                        n += 1
                    dve.wait_ge(tap_v, g * (HALO * len(V_CH)) + n)
                    dve.tensor_copy(pre[:, c, 0:HALO], pre[:, c, GN:GN + HALO]).then_inc(carry_v, 1)
                    if c == 0:
                        if ahead:
                            norm.dve_xn(dve, g + 1)
                        one_plus_e(g)
                    if c == 1:
                        softplus(g)
                    if c == 2:
                        products(g)
                if ahead:
                    norm.dve_lo(dve, g + 1)
                by_token(g)

            over_groups(dve, body)

        @block.gpsimd
        def _(pool):
            pool.memset(pre[:, len(V_CH):XCH, 0:HALO], 0.0).then_inc(carry_p, len(P_CH))
            pool.memset(a0[:, :], 0.0).then_inc(zero_ok, 1)
            pool.wait_ge(w_ok, 1)

            def after(sem, value):
                pool.wait_ge(sem, value)
                pool.sem_inc(seen, 1)

            def body(g, ahead):
                if ahead:
                    norm.pool_rstd(pool, g + 1)
                n = m = 0
                for j, c in enumerate(P_CH):
                    dst = cv[:, c, bass.ds(g * GN, GN)]
                    after(first_ok, g * len(P_CH) + j + 1)
                    pool.tensor_tensor(dst, dst, first[:, j, :], ALU.add).then_inc(tap_p, 1)
                    n += 1
                    for k in range(HALO - 1):
                        after(tap_p, g * (HALO * len(P_CH)) + n)
                        pool.tensor_scalar(prod[:, :], pre[:, c, k:k + GN], cw[:, c, k:k + 1], None,
                                           ALU.mult).then_inc(prod_ok, 1)
                        m += 1
                        after(prod_ok, g * ((HALO - 1) * len(P_CH)) + m)
                        pool.tensor_tensor(dst, dst, prod[:, :], ALU.add).then_inc(tap_p, 1)
                        n += 1
                    after(tap_p, g * (HALO * len(P_CH)) + n)
                    pool.tensor_copy(pre[:, c, 0:HALO], pre[:, c, GN:GN + HALO]).then_inc(carry_p, 1)

            over_groups(pool, body)

        @block.scalar
        def _(act):
            act.sem_inc(ev_ok, EV_FREE)
            act.sem_inc(a_ok, 1)
            act.sem_inc(dttok_ok, 1)
            act.activation(eA[:, :], T["a_log"][:, :], ACT.Exp).then_inc(eA_ok, 1)
            act.wait_ge(w_ok, 1)
            act.wait_ge(A_ok, 1)

            def body(g, ahead):
                for place, c in enumerate(ORDER):
                    act.wait_ge(mm_ok, g * PCH + place + 1)
                    src = bank[place % 4][:, :]
                    if c < 4:
                        act.activation(zs[:, c, bass.ds(g * GN, GN)], src, ACT.Silu, scale=MUP_Z).then_inc(ev_ok, 1)
                    elif c < 4 + XCH:
                        x = c - 4
                        if x in V_CH:
                            act.wait_ge(carry_v, g * len(V_CH) + V_CH.index(x) + 1)
                        else:
                            act.wait_ge(carry_p, g * len(P_CH) + P_CH.index(x) + 1)
                        act.activation(pre[:, x, HALO:HALO + GN], src, ACT.Copy).then_inc(pre_ok, 1)
                        act.activation(cv[:, x, bass.ds(g * GN, GN)], src, ACT.Identity, scale=cw[:, x, HALO:HALO + 1],
                                       bias=cb[:, x:x + 1]).then_inc(ev_ok, 1)
                        if x in P_CH:
                            act.wait_ge(pre_ok, g * XCH + [o - 4 for o in ORDER if 4 <= o < 4 + XCH].index(x) + 1)
                            act.activation(first[:, P_CH.index(x), :], pre[:, x, HALO - 1:HALO - 1 + GN], ACT.Copy,
                                           scale=cw[:, x, HALO - 1:HALO]).then_inc(first_ok, 1)
                    else:
                        act.wait_ge(dt_ok, done(g - 1))
                        for k, r in halves:
                            ins = act.activation(raw[r, :], bank[place % 4][r, H * k:H * k + H], ACT.Identity,
                                                 bias=T["dt_b"][r, 0:1])
                            ins.then_inc(raw_ok, 1)
                        act.wait_ge(raw_ok, g * 2 + 2)
                        act.sem_inc(ev_ok, 1)
                        act.activation(e[:, :], raw[:, :], ACT.Abs).then_inc(abs_ok, 1)
                        act.wait_ge(abs_ok, g + 1)
                        act.activation(e[:, :], e[:, :], ACT.Exp, scale=-1.0).then_inc(exp_ok, 1)
                    if place == 3:
                        act.wait_ge(u_ok, g + 1)
                        act.activation(ln[:, :], u[:, :], ACT.Ln).then_inc(ln_ok, 1)
                    if ahead and place == 7:
                        norm.act_hi(act, g + 1)
                    if place == 5:
                        act.wait_ge(dt_ok, done(g))
                        act.wait_ge(a_sent, g * 32 + 32)
                        act.wait_ge(cp_ok, done(g - 1))
                        act.activation(a[:, :], dt[:, :], ACT.Exp, scale=A[:, 0:1]).then_inc(a_ok, 1)
                    if place == 9:
                        act.wait_ge(tr_dt, done(g))
                        cols = T["dt_tok"][:, :, :].rearrange("p t h -> p (t h)")[:, bass.ds(g * (GT * HEADS),
                                                                                            GT * HEADS)]
                        act.activation(cols.rearrange("p (k t h) -> p k t h", k=2, h=HEADS),
                                       pt_dt[:, :, :].rearrange("p t (k h) -> p k t h", k=2), ACT.Copy
                                       ).then_inc(dttok_ok, 1)

            over_groups(act, body)

        @block.tensor
        def _(pe):
            x_hi, x_lo = norm.xT[:, 0], norm.xT[:, 1]
            pe.sem_inc(tr_dt, 1)
            pe.sem_inc(tr_cp, 1)

            def body(g, ahead):
                for place, c in enumerate(ORDER):
                    last_user = place - 4 if place >= 4 else PCH - 4 + (place + 1) % 4 - PCH
                    pe.wait_ge(ev_ok, g * PCH + max(last_user + 1 + EV_FREE, 1))
                    for kc in range(KC):
                        if place == 0:
                            norm.pe_ready(pe, g, kc)
                        last = split_mm(pe, bank[place % 4][:, :], win[:, 0, kc, c, :], win[:, 1, kc, c, :],
                                        x_hi[:, kc, norm.tokens(g)], x_lo[:, kc, norm.tokens(g)], kc == 0, kc == KC - 1)
                    last.then_inc(mm_ok, 1)
                    if ahead and place == 6:
                        norm.pe_transpose(pe, g + 1)
                    if place == 8:
                        pe.wait_ge(dt_ok, done(g))
                        pe.wait_ge(dttok_ok, done(g - 1))
                        for t in range(HT):
                            last = pe.transpose(pt_dt[:, t, :], dt[:, P * t:P * t + P], T["ident"][:, :])
                        last.then_inc(tr_dt, 1)
                    if place == PCH - 1:
                        pe.wait_ge(dend_ok, g + 1)
                        pe.wait_ge(cpg_ok, done(g - 1))
                        for t in range(HT):
                            pe.transpose(pt_cp[:, t, :], cp[:, P * t:P * t + P], T["ident"][:, :])
                        pe.transpose(pt_cp[0:HB, HT, :], dend[:, :], T["ident"][:, :]).then_inc(tr_cp, 1)

            over_groups(pe, body)

        @block.sync
        def _(sp):
            sp.sem_inc(a_sent, 32)
            sp.sem_inc(dend_sent, 16)
            with sp.Fori(0, GROUPS) as g:
                sp.wait_ge(az_ok, g + 1)
                for k, r in halves:
                    sp.dma_start(T["a_dram"].rearrange("b h i -> h b i")[:, bass.ds(g * (2 * HB) + HB * k, HB), :],
                                 a[r, :].rearrange("h (b i) -> h b i", i=Q)).then_inc(a_sent, 16)
                sp.wait_ge(dendT_ok, g + 1)
                sp.dma_start(T["dend_dram"][bass.ds(g * (2 * HB), 2 * HB), :].rearrange("(k b) h -> b k h", k=2),
                             dendT[:, :].rearrange("b (k h) -> b k h", k=2)).then_inc(dend_sent, 16)
            sp.wait_ge(a_sent, 32 + 32 * GROUPS)
            sp.wait_ge(dend_sent, 16 + 16 * GROUPS)


def build_scan(nc, T):
    with ExitStack() as ctx:
        sb = lambda n, s, d=F32: ctx.enter_context(nc.sbuf_tensor(n, s, d))
        ps = lambda n, s: ctx.enter_context(nc.psum_tensor(n, s, F32))
        sem = lambda n: ctx.enter_context(nc.semaphore(n))
        HI = HEADS * Q
        d0 = [sb(f"d0_{b}", [P, HI]) for b in range(2)]
        dend = [sb(f"dend_{b}", [P, NB, HEADS]) for b in range(2)]
        eye_q = sb("eye_q", [P, HG * Q])
        lmat = sb("lmat", [P, HEADS, Q])
        mmat = sb("mmat", [P, HEADS, Q])
        xbd = sb("xbd", [P, HEADS, NB, PD])
        xT = [sb(f"xs_{b}", [P, 4, P]) for b in range(4)]
        bc = [sb(f"bc_{b}", [P, 2, P]) for b in range(4)]
        xdt, xr, tmp, y, yf, sq, u = (sb(n, [P, INTER]) for n in ("xdt", "xr", "tmp", "y", "yf", "sq", "u"))
        bm = [sb(f"bm_{b}", [P, NB, NS]) for b in range(2)]
        gs = [sb(f"gs_{b}", [P, Q]) for b in range(2)]
        s0 = [sb(f"s0_{b}", [P, INTER]) for b in range(2)]
        s123 = sb("s123", [P, NB - 1, INTER])
        ssum = sb("ssum", [P, P])
        ve = sb("ve_y", [P, 1])
        eps = sb("eps", [P, 1])
        rstd = sb("rstd_y", [P, 1])
        uh = sb("uh", [P, 2, 4, P], F32R)
        X, BG = ps("X", [P, INTER]), ps("BG", [P, NS + Q + 1])
        new = [ps(f"new{b}", [P, INTER]) for b in range(2)]
        intra, yint = ps("intra", [P, NB, HG, PD]), ps("yint", [P, NB, HG * PD])
        ytr, outp = ps("ytr", [P, NB, P]), ps("outp", [P, HID])
        names = ("scan_ok", "smul_ok", "xs_ok", "bc_ok", "tr_ok", "gs_ok", "bm_ok", "xdt_ok", "xbd_ok", "xr_ok",
                 "m_ok", "new_ok", "add_ok", "yint_ok", "intra_ok", "yi_ok", "y_ok", "ytr_ok", "yf_ok", "sq_ok",
                 "u_ok", "uhi_ok", "ulo_ok", "red_ok", "ss_ok", "ve_ok", "rs_ok", "out_ok", "res_ok", "set_ok",
                 "eye_ok", "ma_ok")
        s = {n: sem("c_" + n) for n in names}
        d0_in = [sem(f"d0_in{b}") for b in range(2)]
        dend_in = [sem(f"dend_in{b}") for b in range(2)]
        loaded = sem("ffn_loaded")
        FREE = dict(scan_ok=2, smul_ok=8, m_ok=2, yint_ok=2, new_ok=4, intra_ok=1, xdt_ok=1, bm_ok=4, gs_ok=1,
                    add_ok=2, y_ok=1, yf_ok=16, res_ok=1, xbd_ok=4, ytr_ok=1, sq_ok=1, uhi_ok=1, ss_ok=1,
                    out_ok=1, u_ok=1, ulo_ok=1, red_ok=1, ve_ok=2, ma_ok=2, rs_ok=1)
        PER = dict(smul_ok=4, new_ok=4, bm_ok=4, add_ok=4, xbd_ok=4, yf_ok=4)
        M_ACT = 12
        cv, zs, x_res, wout = T["cv"], T["zs"], T["x_res"], T["wout"]
        block = ctx.enter_context(nc.Block())

        def times(tile, mul):
            i, c = tile
            return c * mul if i is None else i * (4 * mul) + c * mul

        def count(name, tile, after=0, part=0):
            i, c = tile
            per = PER.get(name, 1)
            base = FREE.get(name, 0) + (part if part else per)
            return times((i, c + after), per) + base

        def wait(eng, name, tile, after=0, part=0):
            value = count(name, tile, after, part)
            if tile[0] is not None or value > 0:
                eng.wait_ge(s[name], value)

        def half(tile):
            i, c = tile
            return c // 2 + 1 if i is None else i * 2 + c // 2 + 1

        def pipeline(eng, step):
            for t in range(2):
                step(t, None, True, t >= 1, False)
            with eng.Fori(0, (TILES - 4) // 4) as i:
                for k in range(4):
                    step(2 + k, i, True, True, True)
            for t in range(TILES - 2, TILES + 2):
                step(t, None, t < TILES, t - 1 < TILES, True)

        @block.sync
        def _(sp):
            with sp.Fori(0, TILES // 4) as i:
                for c in range(4):
                    tile = (i, c)
                    wait(sp, "scan_ok", tile, -2)
                    for b in range(NB):
                        src = T["a_dram"].rearrange("b h i -> b (h i)")[bass.ds(i * 16 + c * 4 + b, 1), :]
                        sp.dma_start(d0[c % 2][Q * b:Q * b + Q, :], src.broadcast_to([Q, HI])).then_inc(d0_in[c % 2], 16)
                    wait(sp, "smul_ok", tile, -2)
                    src = T["dend_dram"].rearrange("(t b) h -> t (b h)", b=NB)[bass.ds(i * 4 + c, 1), :]
                    sp.dma_start(dend[c % 2][:, :, :].rearrange("p b h -> p (b h)"),
                                 src.broadcast_to([P, NB * HEADS])).then_inc(dend_in[c % 2], 16)
            wait(sp, "xs_ok", (None, TILES - 1))
            wait(sp, "bc_ok", (None, TILES - 1))
            for name in ("wgu", "wd"):
                chip = T[name][tuple([slice(None)] * len(T[name].shape))].bitcast(F32)
                sp.dma_start(chip, T[name + "_dram"]).then_inc(loaded, 16)
            sp.wait_ge(loaded, 32)

        @block.scalar
        def _(act):
            act.sem_inc(s["bm_ok"], FREE["bm_ok"])
            act.sem_inc(s["gs_ok"], FREE["gs_ok"])
            act.sem_inc(s["xbd_ok"], FREE["xbd_ok"])
            act.sem_inc(s["sq_ok"], FREE["sq_ok"])
            act.sem_inc(s["uhi_ok"], FREE["uhi_ok"])
            act.sem_inc(s["ve_ok"], FREE["ve_ok"])
            act.sem_inc(s["ma_ok"], FREE["ma_ok"])

            def silus(n):
                tok = bass.ds(times(n, P), P)
                wait(act, "yf_ok", n, -4)
                act.activation(xT[n[1] % 4][:, :, :], cv[:, 0:4, tok], ACT.Silu).then_inc(s["xs_ok"], 1)
                wait(act, "yint_ok", n, -4)
                act.activation(bc[n[1] % 4][:, :, :], cv[:, 4:6, tok], ACT.Silu).then_inc(s["bc_ok"], 1)

            def step(c, i, do_a, do_b, do_c):
                a, z = (i, c), (i, c - 2)
                if do_a:
                    wait(act, "tr_ok", a)
                    wait(act, "m_ok", a, -2)
                    act.activation(gs[c % 2][:, :], BG[:, NS:NS + Q], ACT.Copy).then_inc(s["gs_ok"], 1)
                    wait(act, "new_ok", a, -2)
                    if i is None and c == 0:
                        act.wait_ge(s["set_ok"], 3)
                    for b in range(NB):
                        r = slice(Q * b, Q * b + Q)
                        act.activation(bm[c % 2][r, b, :], BG[r, 0:NS], ACT.Copy).then_inc(s["bm_ok"], 1)
                if do_c:
                    wait(act, "yf_ok", z)
                    wait(act, "red_ok", z, -1)
                    act.activation(sq[:, :], yf[:, :], ACT.Square).then_inc(s["sq_ok"], 1)
                    wait(act, "u_ok", z)
                    wait(act, "out_ok", z, -1)
                    act.activation(uh[:, 0, :, :], u[:, :].rearrange("p (g t) -> p g t", g=4), ACT.Copy
                                   ).then_inc(s["uhi_ok"], 1)
                if do_a and (i is not None or c < TILES - 1):
                    silus((i, c + 1))
                if do_c:
                    wait(act, "ss_ok", z)
                    wait(act, "rs_ok", z, -1)
                    act.activation(ve[:, :], BG[:, NS + Q:NS + Q + 1], ACT.Identity, scale=1.0 / INTER,
                                   bias=eps[:, 0:1]).then_inc(s["ve_ok"], 1)
                if do_a:
                    wait(act, "xdt_ok", a)
                    wait(act, "intra_ok", a, -1)
                    if i is None and c == 0:
                        act.wait_ge(s["set_ok"], 4)
                    for b in range(NB):
                        r = slice(Q * b, Q * b + Q)
                        act.activation(xbd[r, :, b, :], xdt[r, :].rearrange("p (h d) -> p h d", d=PD), ACT.Copy
                                       ).then_inc(s["xbd_ok"], 1)
                    wait(act, "gs_ok", a)
                    wait(act, "scan_ok", a)
                    for col in range(Q - M_ACT, Q):
                        ins = act.activation(mmat[:, :, col], lmat[:, :, col], ACT.Copy, scale=gs[c % 2][:, col:col + 1])
                    ins.then_inc(s["ma_ok"], 1)

            silus((None, 0))
            pipeline(act, step)

        @block.vector
        def _(dve):
            for n in ("scan_ok", "xdt_ok", "y_ok", "yf_ok", "res_ok", "u_ok", "ulo_ok", "red_ok"):
                dve.sem_inc(s[n], FREE[n])
            dve.memset(s0[0][:, :], 0.0).then_inc(s["add_ok"], FREE["add_ok"])
            def add(b_, c, b):
                wait(dve, "new_ok", b_, 0, b + 1)
                wait(dve, "smul_ok", b_, 0, b + 1)
                dst = s123[:, b, :] if b < NB - 1 else s0[c % 2][:, :]
                dve.tensor_tensor(dst, tmp[:, :], new[b % 2][:, :], ALU.add).then_inc(s["add_ok"], 1)

            def decay_scan(c, pieces):
                lflat = lmat[:, :, :].rearrange("p h i -> p (h i)")
                for q in pieces:
                    cols = slice(HG * Q * q, HG * Q * (q + 1))
                    ins = dve.tensor_tensor_scan(lflat[:, cols], d0[c % 2][:, cols], eye_q[:, :], 0.0,
                                                 ALU.mult, ALU.add)
                return ins

            def step(c, i, do_a, do_b, do_c):
                a, b_, z = (i, c), (i, c - 1), (i, c - 2)
                if do_a:
                    wait(dve, "tr_ok", a)
                    wait(dve, "xbd_ok", a, -1)
                    wait(dve, "xr_ok", a, -1)
                    dt = T["dt_tok"][:, :, :].rearrange("p t h -> p (t h)")[:, bass.ds(times(a, HEADS), HEADS)]
                    dve.tensor_tensor(xdt[:, :].rearrange("p (h d) -> p h d", d=PD),
                                      X[:, :].rearrange("p (h d) -> p h d", d=PD),
                                      dt.unsqueeze(2).broadcast_to([P, HEADS, PD]), ALU.mult).then_inc(s["xdt_ok"], 1)
                if do_c:
                    wait(dve, "ytr_ok", z)
                    wait(dve, "sq_ok", z, -1)
                    wait(dve, "u_ok", z, -1)
                    for g in range(4):
                        dve.scalar_tensor_tensor(
                            yf[:, P * g:P * g + P].rearrange("p (b t) -> p b t", b=NB),
                            xT[(c - 2) % 4][:, g, :].rearrange("p (b t) -> p b t", b=NB), T["d_ch"][:, g:g + 1],
                            ytr[:, :, Q * g:Q * g + Q], ALU.mult, ALU.add).then_inc(s["yf_ok"], 1)
                    wait(dve, "yf_ok", z)
                    wait(dve, "uhi_ok", z, -1)
                    wait(dve, "ulo_ok", z, -1)
                    dve.tensor_tensor(u[:, :].rearrange("p (g t) -> p g t", g=4),
                                      yf[:, :].rearrange("p (g t) -> p g t", g=4),
                                      zs[:, :, bass.ds(times(z, P), P)], ALU.mult).then_inc(s["u_ok"], 1)
                if do_b:
                    wait(dve, "yint_ok", b_, -1)
                    add(b_, c, 0)
                if do_c:
                    wait(dve, "sq_ok", z)
                    wait(dve, "ss_ok", z, -1)
                    dve.tensor_reduce(ssum[:, :], sq[:, :].rearrange("p (g t) -> p t g", g=4),
                                      mybir.AxisListType.X, ALU.add).then_inc(s["red_ok"], 1)
                    wait(dve, "uhi_ok", z)
                    dve.tensor_tensor(uh[:, 1, :, :].rearrange("p g t -> p (g t)"), u[:, :],
                                      uh[:, 0, :, :].bitcast(F32).rearrange("p g t -> p (g t)"), ALU.subtract
                                      ).then_inc(s["ulo_ok"], 1)
                if do_b:
                    add(b_, c, 1)
                if do_a:
                    dve.wait_ge(d0_in[c % 2], half(a) * (16 * NB))
                    if i is None and c == 0:
                        dve.wait_ge(s["eye_ok"], 2)
                    wait(dve, "m_ok", a, -1)
                    wait(dve, "ma_ok", a, -1)
                    decay_scan(c, (0, 1))
                if do_b:
                    add(b_, c, 2)
                if do_a:
                    decay_scan(c, (2, 3)).then_inc(s["scan_ok"], 1)
                if do_b:
                    add(b_, c, 3)
                if do_a:
                    wait(dve, "xdt_ok", a)
                    wait(dve, "scan_ok", a)
                    wait(dve, "new_ok", a, -1)
                    dve.tensor_tensor(xr[:, :].rearrange("p (h d) -> p h d", d=PD),
                                      xdt[:, :].rearrange("p (h d) -> p h d", d=PD),
                                      lmat[:, :, Q - 1:Q].broadcast_to([P, HEADS, PD]), ALU.mult
                                      ).then_inc(s["xr_ok"], 1)
                if do_b:
                    wait(dve, "yint_ok", b_)
                    wait(dve, "ytr_ok", b_, -1)
                    cp = T["cp_g"][:, :, :, :].rearrange("p t b h -> p (t b h)")[:, bass.ds(times(b_, HEADS), HEADS)]
                    dve.tensor_tensor(y[:, :].rearrange("p (h d) -> p h d", d=PD),
                                      yint[:, :, :].rearrange("p b (h d) -> p (b h) d", d=PD),
                                      cp.unsqueeze(2).broadcast_to([P, HEADS, PD]), ALU.mult).then_inc(s["yi_ok"], 1)
                    wait(dve, "yi_ok", b_)
                    wait(dve, "intra_ok", b_)
                    dve.tensor_tensor(y[:, :], y[:, :], intra[:, :, :, :].rearrange("p b h d -> p (b h d)"),
                                      ALU.add).then_inc(s["y_ok"], 1)
                if do_c:
                    wait(dve, "out_ok", z)
                    wait(dve, "rs_ok", z)
                    xt = x_res[:, :, :].rearrange("p t c -> p (t c)")[:, bass.ds(times(z, HID), HID)]
                    dve.scalar_tensor_tensor(xt, outp[:, :], rstd[:, 0:1], xt, ALU.mult, ALU.add
                                             ).then_inc(s["res_ok"], 1)

            pipeline(dve, step)

        @block.gpsimd
        def _(pool):
            pool.sem_inc(s["smul_ok"], FREE["smul_ok"])
            pool.sem_inc(s["m_ok"], FREE["m_ok"])
            pool.sem_inc(s["rs_ok"], FREE["rs_ok"])
            pool.memset(eps[:, :], EPS).then_inc(s["set_ok"], 1)
            for b in range(2):
                pool.memset(bm[b][:, :, :], 0.0).then_inc(s["set_ok"], 1)
            pool.memset(eye_q[:, :], 0.0).then_inc(s["eye_ok"], 1)
            pool.memset(xbd[:, :, :, :], 0.0).then_inc(s["set_ok"], 1)
            pool.wait_ge(s["eye_ok"], 1)
            pool.wait_ge(s["set_ok"], 4)
            for b in range(NB):
                part = eye_q[Q * b:Q * b + Q, :].rearrange("p (h i) -> p h i", i=Q)
                ins = pool.affine_select(out=part, in_=part, compare_op=ALU.not_equal, fill=1.0, base=0,
                                         pattern=[[0, HG], [-1, Q]], channel_multiplier=1)
            ins.then_inc(s["eye_ok"], 1)

            def step(c, i, do_a, do_b, do_c):
                a, b_, z = (i, c), (i, c - 1), (i, c - 2)
                if do_b:
                    pool.wait_ge(dend_in[(c - 1) % 2], half(b_) * 16)
                    for b in range(NB):
                        wait(pool, "add_ok", b_, 0, b) if b else wait(pool, "add_ok", b_, -1)
                        src = s0[(c - 1) % 2][:, :] if b == 0 else s123[:, b - 1, :]
                        pool.tensor_tensor(tmp[:, :].rearrange("p (h d) -> p h d", d=PD),
                                           src.rearrange("p (h d) -> p h d", d=PD),
                                           dend[(c - 1) % 2][:, b, :].unsqueeze(2).broadcast_to([P, HEADS, PD]),
                                           ALU.mult).then_inc(s["smul_ok"], 1)
                if do_c:
                    wait(pool, "ve_ok", z)
                    wait(pool, "res_ok", z, -1)
                    pool.tensor_tensor(rstd[:, :], ve[:, :], T["m_half"][:, 0:1], ALU.pow).then_inc(s["rs_ok"], 1)
                if do_a:
                    wait(pool, "scan_ok", a)
                    wait(pool, "gs_ok", a)
                    wait(pool, "intra_ok", a, -1)
                    cols = slice(0, Q - M_ACT)
                    pool.tensor_tensor(mmat[:, :, cols], lmat[:, :, cols],
                                       gs[c % 2][:, cols].unsqueeze(1).broadcast_to([P, HEADS, Q - M_ACT]), ALU.mult
                                       ).then_inc(s["m_ok"], 1)

            pipeline(pool, step)

        @block.tensor
        def _(pe):
            for n in ("yint_ok", "new_ok", "intra_ok", "ytr_ok", "ss_ok", "out_ok"):
                pe.sem_inc(s[n], FREE[n])

            def new_state(b_, c, b):
                pe.wait_ge(s["add_ok"], times(b_, NB) + b + 1)
                pe.matmul(new[b % 2][:, :], bm[(c - 1) % 2][:, b, :], xr[:, :], start=True, stop=True
                          ).then_inc(s["new_ok"], 1)

            def intra_heads(heads):
                for hh in heads:
                    for g in range(4):
                        h = HG * g + hh
                        ins = pe.matmul(intra[Q * g:Q * g + Q, :, hh, :], mmat[:, h, :], xbd[:, h, :, :],
                                        start=True, stop=True)
                return ins

            def step(c, i, do_a, do_b, do_c):
                a, b_, z = (i, c), (i, c - 1), (i, c - 2)
                if do_a:
                    wait(pe, "xs_ok", a)
                    wait(pe, "xdt_ok", a, -1)
                    for g in range(4):
                        pe.transpose(X[:, P * g:P * g + P], xT[c % 4][:, g, :], T["ident"][:, :])
                    wait(pe, "bc_ok", a)
                    wait(pe, "bm_ok", a, -1)
                    wait(pe, "gs_ok", a, -1)
                    wait(pe, "ve_ok", a, -3)
                    pe.transpose(BG[:, 0:NS], bc[c % 4][:, 0, :], T["ident"][:, :])
                    for b in range(NB):
                        r = slice(Q * b, Q * b + Q)
                        ins = pe.matmul(BG[r, NS:NS + Q], bc[c % 4][:, 0, r], bc[c % 4][:, 1, r], start=True, stop=True)
                    ins.then_inc(s["tr_ok"], 1)
                if do_c:
                    wait(pe, "y_ok", z)
                    wait(pe, "yf_ok", z, -1)
                    for b in range(NB):
                        ins = pe.transpose(ytr[:, b, :], y[:, P * b:P * b + P], T["ident"][:, :])
                    ins.then_inc(s["ytr_ok"], 1)
                if do_b:
                    wait(pe, "xr_ok", b_)
                    wait(pe, "bm_ok", b_)
                    new_state(b_, c, 0)
                    new_state(b_, c, 1)
                    wait(pe, "m_ok", b_)
                    wait(pe, "ma_ok", b_)
                    wait(pe, "xbd_ok", b_)
                    wait(pe, "y_ok", b_, -1)
                    intra_heads(range(0, 12))
                    new_state(b_, c, 2)
                if do_c:
                    wait(pe, "red_ok", z)
                    if do_a:
                        wait(pe, "bm_ok", a)
                    pe.matmul(BG[:, NS + Q:NS + Q + 1], ssum[:, :], T["ones"][:, 0:1], start=True, stop=True
                              ).then_inc(s["ss_ok"], 1)
                if do_b:
                    new_state(b_, c, 3)
                    intra_heads(range(12, HG)).then_inc(s["intra_ok"], 1)
                    for b in range(NB):
                        wait(pe, "add_ok", b_, 0, b) if b else wait(pe, "add_ok", b_, -1)
                        st = s0[(c - 1) % 2] if b == 0 else s123[:, b - 1, :]
                        for g in range(4):
                            ins = pe.matmul(yint[Q * g:Q * g + Q, b, :], bc[(c - 1) % 4][:, 1, Q * b:Q * b + Q],
                                            st[:, P * g:P * g + P], start=True, stop=True)
                    ins.then_inc(s["yint_ok"], 1)
                if do_c:
                    wait(pe, "ulo_ok", z)
                    wait(pe, "res_ok", z, -1)
                    for k in range(4):
                        ins = split_mm(pe, outp[:, :], uh[:, 0, k, :], uh[:, 1, k, :], wout[:, 0, k, :],
                                       wout[:, 1, k, :], k == 0, k == 3)
                    ins.then_inc(s["out_ok"], 1)

            pipeline(pe, step)


def build(nc, A, out):
    T = {}
    for name, shape, dt in (("a_dram", (BLOCKS, HEADS, Q), F32), ("dend_dram", (BLOCKS, HEADS), F32),
                            ("wgu_dram", (P, 2, KC, GUC, P), F32), ("wd_dram", (P, 2, FCH, HID), F32)):
        T[name] = nc.dram_tensor(name, shape, dt, kind="Internal").ap()
    with ExitStack() as base:
        def put(stack, *tensors, side="left"):
            for name, shape, *dt in tensors:
                T[name] = stack.enter_context(nc.sbuf_tensor(f"{name}_{len(T)}", shape, (dt or [F32])[0], side=side))

        put(base, ("x_res", [P, TILES, HID]), ("wout", [P, 2, 4, HID], F32R), ("ident", [P, P]), ("ones", [P, 1]),
            ("m_half", [P, GT]), ("norm_w", [P, 4]), ("conv_b", [P, XCH]), ("conv_w", [P, XCH, KCONV]),
            ("a_log", [P, 1]), ("dt_b", [P, 1]), ("d_ch", [P, 4]))
        ffn_w = (("wgu", [P, 2, KC, GUC, P], F32R), ("wd", [P, 2, FCH, HID], F32R))
        with ExitStack() as win_s:
            norm = Norm(nc, win_s, T, "n1_", side="right")
            put(win_s, ("win", [P, 2, KC, PCH, P], F32R), side="right")
            with ExitStack() as ffn1:
                put(ffn1, *ffn_w)
                build_weights(nc, T, A, norm)
                build_ffn(nc, T, "f1_", norm)
            mamba = ExitStack()
            put(mamba, ("cv", [P, XCH, L]), ("zs", [P, 4, L]), ("dt_tok", [P, TILES, HEADS]),
                ("cp_g", [P, TILES, NB, HG]))
            build_in_proj(nc, T, norm)
        build_scan(nc, T)
        mamba.close()
        with ExitStack() as ffn2:
            for name, shape, dt in ffn_w:
                ffn2.enter_context(nc.sbuf_tensor(name + "_again", shape, dt))
            build_ffn(nc, T, "f2_", Norm(nc, ffn2, T, "n2_"), out)


_INS = dict(x="L0_attn_hidden_states", in_w="L0_attn_in_proj_w", conv_w="L0_attn_conv_w", conv_b="L0_attn_conv_b",
            A_log="L0_attn_A_log", D="L0_attn_D", dt_bias="L0_attn_dt_bias", norm_w="L0_attn_norm_w",
            out_w="L0_attn_out_proj_w", lut="L0_ffn_lut", gate="L0_ffn_gate_idx", up="L0_ffn_up_idx",
            down="L0_ffn_down_idx")


def kernel(**inputs):
    import numpy as _np
    import concourse.bacc as _bacc
    from concourse.bass_utils import run_bass_kernel_spmd as _run

    nc = _bacc.Bacc("TRN2", target_bir_lowering=False, num_devices=1)
    arrays, args = {}, {}
    for short, name in _INS.items():
        a = _np.ascontiguousarray(inputs[name])
        arrays[f"in_{short}"] = a
        args[short] = nc.dram_tensor(f"in_{short}", a.shape, mybir.dt.from_np(a.dtype), kind="ExternalInput").ap()
    out = nc.dram_tensor("out_0", (1, L, HID), F32, kind="ExternalOutput").ap()
    build(nc, args, out)
    return _run(nc, [arrays], core_ids=[0]).results[0]["out_0"]
```
